# Optimizing a Trainium2 kernel written in Bass

```python
import numpy as np
import jax
import jax.numpy as jnp

def _softmax(x, axis=-1):
    return jax.nn.softmax(x, axis=axis)

def _gelu(x):
    return jax.nn.gelu(x, approximate=True)

def _silu(x):
    return jax.nn.silu(x)

def _sigmoid(x):
    return jax.nn.sigmoid(x)

def _layernorm(x, axis=-1, eps=1e-05):
    m = jnp.mean(x, axis=axis, keepdims=True)
    v = jnp.var(x, axis=axis, keepdims=True)
    return (x - m) / jnp.sqrt(v + eps)

def _scatter_add(tgt, idx, src, axis=0):
    return tgt.at[idx].add(src)

def _segment_sum(src, seg, n):
    return jax.ops.segment_sum(src, seg, n)
kernel_name = 'mk_flamingo_gated_d1_seqx_r4_79ccb0'

def setup_inputs(seed: int=0):
    np.random.seed(seed)
    _w = jnp.asarray

    def _rec_inputs():
        import jax
        import jax.numpy as jnp
        _rk = jax.random.key(seed)
        x = 7.22e-05 + 1 * jax.random.normal(jax.random.fold_in(_rk, 1), (16, 256, 512), jnp.float32)
        _lenS = 256 - jax.random.randint(jax.random.fold_in(_rk, 7), (16,), 0, max(1, 256 // 4) + 1, jnp.int32)
        _lenS2 = 256 - jax.random.randint(jax.random.fold_in(_rk, 8), (16,), 0, max(1, 256 // 4) + 1, jnp.int32)
        _ctx_512P = jax.random.normal(jax.random.fold_in(_rk, 11), (16, 16, 128), jnp.float32)
        _ctx_512c = jax.random.dirichlet(jax.random.fold_in(_rk, 511), 0.3 * jnp.ones((16,), jnp.float32), (16, 256))
        _ctx_512t = jnp.einsum('bsk,bkd->bsd', _ctx_512c, _ctx_512P)
        _ctx_512t = _ctx_512t * jax.lax.rsqrt(jnp.mean(jnp.square(_ctx_512t)) + 1e-12) * 0.953939
        ctx_512 = -0.000514642 + 1.00011 * (_ctx_512t + 0.3 * jax.random.normal(jax.random.fold_in(_rk, 611), (16, 256, 128), jnp.float32))
        _g = jax.random.normal(jax.random.fold_in(_rk, 9001), (2, 1), jnp.float32)
        _g = jnp.sign(_g) * jnp.maximum(jnp.abs(_g), 1.0) + (_g == 0) * 1.0
        g_xattn = _g[0]
        g_ffn = _g[1]
        return (x, ctx_512, g_xattn, g_ffn)
    x, ctx_512, g_xattn, g_ffn = _rec_inputs()

    def _L0_xattn_setup():
        import jax, jax.numpy as jnp
        import numpy as np
        B, S, H, NH, L = (2, 512, 512, 16, 128)
        HD = H // NH
        key = jax.random.key(seed)
        k1, k2, k3, k4, k5 = jax.random.split(key, 5)
        scale = 0.02
        return {'q': jax.random.normal(k1, (B, S, H), dtype=jnp.float32), 'latent_kv': jax.random.normal(k2, (B, S, L), dtype=jnp.float32), 'Wq': jax.random.normal(k3, (H, H), dtype=jnp.float32) * scale, 'Wkv_expand': jax.random.normal(k4, (2 * H, L), dtype=jnp.float32) * scale, 'Wout': jax.random.normal(k5, (H, H), dtype=jnp.float32) * scale}
    _L0_xattn_all = _L0_xattn_setup()
    _L0_xattn_in = {k: v for k, v in _L0_xattn_all.items() if k in ('Wq', 'Wkv_expand', 'Wout')}
    del _L0_xattn_all

    def _L0_ffn_setup():
        import jax, jax.numpy as jnp
        import numpy as np
        FP8_MAX = 448.0
        GLOBAL_DIV = 448.0 * 6.0

        def _fp8(x):
            return x.astype(jnp.float8_e4m3fn).astype(jnp.float32)

        def _reorder_quantize_x(x, idx):
            scale = jnp.max(jnp.abs(x)) / GLOBAL_DIV
            xr = (x / scale)[:, idx]
            scale_x = jnp.max(jnp.abs(xr), axis=1, keepdims=True) / FP8_MAX
            qx = _fp8(xr / scale_x)
            return (qx, scale_x, scale)

        def _qlinear(qx, scale_x, scale, W, idx, out_idx=None):
            Wr = W[:, idx]
            w_scale = jnp.max(jnp.abs(Wr), axis=1, keepdims=True) / FP8_MAX
            qw = _fp8(Wr / w_scale)
            y = qx * scale_x @ (qw * w_scale).T * scale
            if out_idx is not None:
                y = y[:, out_idx]
            return y
        key = jax.random.key(seed)
        ks = jax.random.split(key, 6)
        B, S, H, I = (2, 256, 512, 1408)
        return {'x': jax.random.normal(ks[0], (B, S, H), jnp.float32), 'w_gate': jax.random.normal(ks[1], (I, H), jnp.float32) * 0.02, 'w_up': jax.random.normal(ks[2], (I, H), jnp.float32) * 0.02, 'w_down': jax.random.normal(ks[3], (H, I), jnp.float32) * 0.02, 'up_reorder_index': jax.random.permutation(ks[4], jnp.arange(H, dtype=jnp.int64)), 'down_reorder_index': jax.random.permutation(ks[5], jnp.arange(I, dtype=jnp.int64))}
    _L0_ffn_all = _L0_ffn_setup()
    _L0_ffn_in = {k: v for k, v in _L0_ffn_all.items() if k in ('w_gate', 'w_up', 'w_down', 'up_reorder_index', 'down_reorder_index')}
    del _L0_ffn_all
    return {'x': x, 'ctx_512': ctx_512, 'g_xattn': g_xattn, 'g_ffn': g_ffn, 'L0_xattn_Wq': _L0_xattn_in['Wq'], 'L0_xattn_Wkv_expand': _L0_xattn_in['Wkv_expand'], 'L0_xattn_Wout': _L0_xattn_in['Wout'], 'L0_ffn_w_gate': _L0_ffn_in['w_gate'], 'L0_ffn_w_up': _L0_ffn_in['w_up'], 'L0_ffn_w_down': _L0_ffn_in['w_down'], 'L0_ffn_up_reorder_index': _L0_ffn_in['up_reorder_index'], 'L0_ffn_down_reorder_index': _L0_ffn_in['down_reorder_index']}

def reference(x, ctx_512, g_xattn, g_ffn, L0_xattn_Wq, L0_xattn_Wkv_expand, L0_xattn_Wout, L0_ffn_w_gate, L0_ffn_w_up, L0_ffn_w_down, L0_ffn_up_reorder_index, L0_ffn_down_reorder_index):
    import jax
    import jax.numpy as jnp

    def _L0_xattn_ref(q, latent_kv, Wq, Wkv_expand, Wout):
        import jax, jax.numpy as jnp
        import numpy as np
        B, S, H, NH, L = (2, 512, 512, 16, 128)
        HD = H // NH
        b, sq, _ = q.shape
        sk = latent_kv.shape[1]
        qp = q @ Wq.T
        kv = latent_kv @ Wkv_expand.T
        k, v = jnp.split(kv, 2, axis=-1)
        qh = qp.reshape(b, sq, NH, HD).transpose(0, 2, 1, 3)
        kh = k.reshape(b, sk, NH, HD).transpose(0, 2, 1, 3)
        vh = v.reshape(b, sk, NH, HD).transpose(0, 2, 1, 3)
        inv_sqrt_d = 1.0 / jnp.sqrt(jnp.float32(HD))
        scores = jnp.einsum('bhqd,bhkd->bhqk', qh, kh) * inv_sqrt_d
        causal = jnp.tril(jnp.ones((sq, sk), dtype=bool))
        scores = jnp.where(causal, scores, jnp.finfo(scores.dtype).min)
        attn = jax.nn.softmax(scores, axis=-1)
        out = jnp.einsum('bhqk,bhkd->bhqd', attn, vh)
        out = out.transpose(0, 2, 1, 3).reshape(b, sq, H)
        return out @ Wout.T

    def _L0_ffn_ref(x, w_gate, w_up, w_down, up_reorder_index, down_reorder_index):
        import jax, jax.numpy as jnp
        import numpy as np
        FP8_MAX = 448.0
        GLOBAL_DIV = 448.0 * 6.0

        def _fp8(x):
            return x.astype(jnp.float8_e4m3fn).astype(jnp.float32)

        def _reorder_quantize_x(x, idx):
            scale = jnp.max(jnp.abs(x)) / GLOBAL_DIV
            xr = (x / scale)[:, idx]
            scale_x = jnp.max(jnp.abs(xr), axis=1, keepdims=True) / FP8_MAX
            qx = _fp8(xr / scale_x)
            return (qx, scale_x, scale)

        def _qlinear(qx, scale_x, scale, W, idx, out_idx=None):
            Wr = W[:, idx]
            w_scale = jnp.max(jnp.abs(Wr), axis=1, keepdims=True) / FP8_MAX
            qw = _fp8(Wr / w_scale)
            y = qx * scale_x @ (qw * w_scale).T * scale
            if out_idx is not None:
                y = y[:, out_idx]
            return y
        B, S, H = x.shape
        xf = x.reshape(B * S, H)
        qx, sx, sc = _reorder_quantize_x(xf, up_reorder_index)
        g = _qlinear(qx, sx, sc, w_gate, up_reorder_index, out_idx=down_reorder_index)
        u = _qlinear(qx, sx, sc, w_up, up_reorder_index, out_idx=down_reorder_index)
        t = jax.nn.silu(g) * u
        qt, st, sct = _reorder_quantize_x(t, down_reorder_index)
        y = _qlinear(qt, st, sct, w_down, down_reorder_index)
        return y.reshape(B, S, H)
    x = x + jnp.tanh(g_xattn[0]) * _L0_xattn_ref(_layernorm(x, axis=-1), ctx_512, L0_xattn_Wq, L0_xattn_Wkv_expand, L0_xattn_Wout)
    x = x + jnp.tanh(g_ffn[0]) * _L0_ffn_ref(_layernorm(x, axis=-1), L0_ffn_w_gate, L0_ffn_w_up, L0_ffn_w_down, L0_ffn_up_reorder_index, L0_ffn_down_reorder_index)
    return x

_drawn_inputs = setup_inputs


def setup_inputs(seed=0):
    import zlib

    import numpy as np

    out = dict(_drawn_inputs(seed))
    spreads = {}
    factors = {'L0_xattn_Wq': 31.636}
    for name, (base, spread) in spreads.items():
        noise = np.random.default_rng([zlib.crc32(name.encode()), seed]).standard_normal(out[name].shape)
        drawn = base * np.exp(spread * noise) if base else spread * noise
        out[name] = jnp.asarray(drawn.astype(out[name].dtype))
    for name, factor in factors.items():
        out[name] = (out[name] * factor).astype(out[name].dtype)
    return out
```

```python
from contextlib import ExitStack

import concourse.bass as bass
from concourse import mybir

P = 128
FP8_MAX = 448.0
ROUND_FLOOR = 1.5 * 2.0**-6
ROUND_LIFT = 2.0**20
LN_EPS = 1e-5
MASKED = -3.3e38

F32 = mybir.dt.float32
BF16 = mybir.dt.bfloat16
U32 = mybir.dt.uint32
ALU = mybir.AluOpType
ACT = mybir.ActivationFunctionType
AX = mybir.AxisListType


class Progress:

    def __init__(self, sem, steps):
        self.sem = sem
        self.steps = list(steps)
        self.at = 0

    def done(self, instruction, step):
        assert self.steps[self.at % len(self.steps)] == step, (step, self.steps[self.at % len(self.steps)])
        self.at += 1
        instruction.then_inc(self.sem, 1)

    def wait(self, eng, step, b):
        value = b * len(self.steps) + self.steps.index(step) + 1
        if isinstance(value, int) and value <= 0:
            return
        eng.wait_ge(self.sem, value)


class Loads:

    def __init__(self, sem, n):
        self.sem = sem
        self.n = n

    def started(self, dma):
        dma.then_inc(self.sem, 16)

    def wait(self, eng, b):
        value = (b + 1) * (16 * self.n)
        if isinstance(value, int) and value <= 0:
            return
        eng.wait_ge(self.sem, value)


def names(prefix, n):
    return [f"{prefix}{i}" for i in range(n)]


def gated_block_kernel(nc, x, ctx_in, g_x, g_f, w_q, w_kv, w_out, w_gate, w_up, w_down, down_index, out):
    NB, S, H = x.shape
    L = ctx_in.shape[2]
    I = w_gate.shape[0]
    HD = 32
    NH = H // HD
    TT = S // P
    KT = H // P
    IT = I // P
    G = P // HD
    NC = NH // 2
    SCALE = float(HD) ** -0.5
    assert (TT, L, KT * P, IT * P) == (2, P, H, I) and KT == 4 and G == 4

    with ExitStack() as stack:
        def sb(name, shape, dt=F32):
            return stack.enter_context(nc.sbuf_tensor(name, shape, dt))

        def sem(name):
            return stack.enter_context(nc.semaphore(name))

        att = [stack.enter_context(nc.psum_tensor(f"att{i}", [P, 1024], F32)) for i in range(2)]
        wk = [stack.enter_context(nc.psum_tensor(f"wk{i}", [P, 512], F32)) for i in range(2)]
        ff = [stack.enter_context(nc.psum_tensor(f"ff{i}", [P, 512], F32)) for i in range(2)]

        ident = sb("ident", [P, P])
        identb = sb("identb", [P, P], BF16)
        ones = sb("ones", [P, P])
        causal4 = sb("causal4", [P, 4, P], BF16)
        pick = sb("pick", [P, KT, HD])
        minus_half = sb("minus_half", [P, TT])
        gates = sb("gates", [1, 2])
        tanh_g = sb("tanh_g", [P, 2])
        index = sb("index", [P, IT], mybir.dt.int32)

        WqTh = sb("WqTh", [P, KT, H], BF16)
        WqTl = sb("WqTl", [P, KT, H], BF16)
        WkvTh = sb("WkvTh", [P, 2 * H], BF16)
        WkvTl = sb("WkvTl", [P, 2 * H], BF16)
        WoTh = sb("WoTh", [P, KT, H], BF16)
        WoTl = sb("WoTl", [P, KT, H], BF16)
        WgT = sb("WgT", [P, KT, I], BF16)
        WuT = sb("WuT", [P, KT, I], BF16)
        WdT = sb("WdT", [P, IT, H], BF16)
        wscale = sb("wscale", [P, 3, IT])
        wmax = sb("wmax", [P, 3, IT])
        winv = sb("winv", [P, 3, IT])
        down_scale = sb("down_scale", [P, H])

        xin = sb("xin", [P, TT, H])
        cin = sb("cin", [P, TT, L])
        xres = sb("xres", [P, TT, H])
        bn = sb("bn", [P, TT, 6])
        mv = sb("mv", [P, TT, 2])
        var_eps = sb("var_eps", [P, TT])
        rstd = sb("rstd", [P, TT])
        xn = sb("xn", [P, TT, H])
        xTh = sb("xTh", [P, KT, S], BF16)
        xTl = sb("xTl", [P, KT, S], BF16)
        cTh = sb("cTh", [P, S], BF16)
        cTl = sb("cTl", [P, S], BF16)
        kh = sb("kh", [P, KT, S], BF16)
        kl = sb("kl", [P, KT, S], BF16)
        qh = sb("qh", [P, KT, S], BF16)
        ql = sb("ql", [P, KT, S], BF16)
        V = sb("V", [P, TT, H])
        Q4 = sb("Q4", [P, NH, S], BF16)
        K4 = sb("K4", [P, NH, S], BF16)
        mx = sb("mx", [P, TT, NH])
        m_parts = sb("m_parts", [P, 3, TT * NH], BF16)
        m_rest = sb("m_rest", [P, 2, TT * NH])
        mT = sb("mT", [3 * TT * NH, P], BF16)
        PT = sb("PT", [P, NC, 768])
        O = sb("O", [P, KT, S])
        rsum = sb("rsum", [P, S])
        R = sb("R", [P, KT, S])
        oh = sb("oh", [P, KT, S], BF16)
        ol = sb("ol", [P, KT, S], BF16)
        x1 = sb("x1", [P, TT, H])
        bn2 = sb("bn2", [P, TT, 6])
        mv2 = sb("mv2", [P, TT, 2])
        var_eps2 = sb("var_eps2", [P, TT])
        rstd2 = sb("rstd2", [P, TT])
        amax = sb("amax", [P, TT])
        ainv = sb("ainv", [P, TT])
        sx = sb("sx", [P, TT])
        T = sb("T", [P, IT, S])
        dq = sb("dq", [P, 2, IT, S], BF16)
        tmax = sb("tmax", [P, 2, S])
        tm = sb("tm", [P, TT])
        tinv = sb("tinv", [P, TT])
        st = sb("st", [P, TT])
        ob = sb("ob", [P, TT, H])

        raw_a = sb("raw_a", [P, IT * H])
        carved = [0]

        def carve(a, n, dt=F32):
            words = a * n * (2 if dt == BF16 else 4) // 4
            at, carved[0] = carved[0], carved[0] + words
            part = raw_a[:, at:at + words]
            part = part.bitcast(dt) if dt == BF16 else part
            return part.rearrange("p (a n) -> p a n", a=a)

        cx = carve(TT, H)
        dx = carve(TT, H, BF16)
        qx = carve(TT, H, BF16)
        qxT = carve(KT, S, BF16)
        gs = carve(2, S)
        sl = carve(2, S)
        yb = carve(TT, H)
        spread = carve(TT, P)
        spread2 = carve(TT, P)
        sxb = raw_a[:, carved[0]:carved[0] + S]
        tinvb = raw_a[:, carved[0] + S:carved[0] + 2 * S]
        assert carved[0] + 2 * S <= IT * H
        raw_q = PT[:, :, :].rearrange("p c n -> p (c n)")[:, 0:KT * H].rearrange("p (m h) -> p m h", m=KT)
        raw_kv = xn[:, :, :].rearrange("p t h -> p (t h)").rearrange("p (m l) -> p m l", l=L)
        raw_o = raw_a[:, 0:KT * H].rearrange("p (m h) -> p m h", m=KT)
        raw_gate = raw_a[:, :]
        raw_up = PT[:, :, :].rearrange("p c n -> p (c n)")[:, 0:IT * H]
        raw_down = raw_a[:, :]
        wd = T[:, :, :].bitcast(BF16).rearrange("p i s -> p (i s)")
        wq8 = dq[:, :, :, :].rearrange("p a i s -> p (a i s)")

        s_const = sem("s_const")
        s_index = sem("s_index")
        s_apart = sem("s_apart")
        s_gates = sem("s_gates")
        s_raw = [sem(f"s_raw_{n}") for n in ("q", "kv", "o", "gate", "up", "down")]
        peW = Progress(sem("peW"), ["g"] + names("a", 10))
        actW = Progress(sem("actW"), ["tanh"] + names("a", 10))
        dveW = Progress(sem("dveW"), names("a", 10))
        w_steps = [s + str(j) for j in range(3) for s in ("mx", "rc", "iv", "sc", "x", "d", "y", "q")]
        dveF = Progress(sem("dveF"), w_steps + ["spread", "dsc"])
        peF = Progress(sem("peF"), names("t", 18) + ["sc"])
        actF = Progress(sem("actF"), ["abs0", "abs1"] + names("t", 6) + ["abs2"] + [f"t{n}" for n in range(6, 18)])

        load_x = Loads(sem("load_x"), 2)
        load_res = Loads(sem("load_res"), 1)
        stack_k = Loads(sem("stack_k"), 12)
        stack_q = Loads(sem("stack_q"), 13)
        stack_m = Loads(sem("stack_m"), 6)
        store = Loads(sem("store"), 1)

        proj = ["xT0", "xT1", "cT", "k0", "k1", "v0", "v1", "q0", "q1"]
        peA = Progress(sem("peA"), proj + names("S", NC) + ["mT", "ST0", "ST1", "ST2", "PV0", "ST3", "ST4", "PV1",
                                                            "ST5", "ST6", "PV2", "ST7", "PV3", "sum", "wo0", "wo1"])
        peB = Progress(sem("peB"), ["qxT", "sxb"] + names("gu", IT) + ["amT", "invb", "dn0", "dn1"])
        dveP = Progress(sem("dveP"), ["st0", "st1", "ag0", "ag1", "xn0", "xn1"])
        dveA = Progress(sem("dveA"), ["xT0", "xT1", "cT", "k0", "k1", "q0", "q1"]
                        + [f"mx{c}{h}" for c in range(NC) for h in "ab"]
                        + ["m1", "r1", "m2", "m3", "rc"] + names("sh", KT) + ["on", "ol", "x1_0", "x1_1"])
        dveB = Progress(sem("dveB"), ["st0", "st1", "ag0", "ag1", "c0", "c1", "am", "sx0", "sx1", "rc", "iv", "x0", "x1",
                                      "d", "y", "q", "sp0", "sp1"]
                        + mlp_steps(IT) + ["mt", "st_a", "st_b", "rc2", "iv2", "sq0", "sq1", "X", "D", "Y", "Q", "y0", "y1"])
        actA = Progress(sem("actA"), proj + ["mT", "e0", "e1", "e2", "O0", "e3", "e4", "O1", "e5", "e6", "O2", "e7", "O3", "oh"])
        actB = Progress(sem("actB"), ["absx", "qxT", "sxb"] + names("silu", IT) + ["invb", "absT"])
        poolP = Progress(sem("poolP"), ["ve", "rs"])
        poolA = Progress(sem("poolA"), [f"sel{c}{h}" for c in range(NC) for h in "ab"])
        poolB = Progress(sem("poolB"), ["ve", "rs", "o0", "o1"])

        wk_uses = proj + ["mT", "PV0", "PV1", "PV2", "PV3", "sum", "wo0", "wo1"]
        wk_freed = {n: (dveA, n) for n in proj if n[0] != "v"}
        wk_freed |= {"v0": (actA, "v0"), "v1": (actA, "v1"), "mT": (actA, "mT"), "sum": (dveA, "rc")}
        wk_freed |= {f"PV{g}": (actA, f"O{g}") for g in range(KT)} | {f"wo{t}": (dveA, f"x1_{t}") for t in range(TT)}
        ff_uses = ["qxT", "sxb"] + names("gu", IT) + ["amT", "invb", "dn0", "dn1"]
        ff_freed = {"qxT": (actB, "qxT"), "sxb": (actB, "sxb"), "amT": (dveB, "mt"), "invb": (actB, "invb"),
                    "dn0": (dveB, "y0"), "dn1": (dveB, "y1")} | {f"gu{n}": (dveB, f"t{n}") for n in range(IT)}

        def bank(banks, uses, freed, use, eng=None, b=None):
            n = uses.index(use)
            if eng is not None:
                before = uses[n - 2]
                before, lag = (uses[n - 2], 0) if n >= 2 else (uses[len(uses) - 1 - n], 1)
                progress, step = freed[before]
                progress.wait(eng, step, b - lag)
            return banks[n % 2]

        assert len(wk_uses) % 2 == 1 and len(ff_uses) % 2 == 1

        def wkb(use, eng=None, b=None):
            return bank(wk, wk_uses, wk_freed, use, eng, b)

        def ffb(use, eng=None, b=None):
            return bank(ff, ff_uses, ff_freed, use, eng, b)

        N_CONST = 9 + 3 + KT

        def apart(eng):
            eng.sem_inc(s_apart, 1)

        block = stack.enter_context(nc.Block())

        def pipeline(eng, iteration):
            iteration(1, 0, None)
            iteration(2, 1, 0)
            with eng.Fori(2, NB - 1) as i:
                iteration(i + 1, i, i - 1)
            iteration(None, NB - 1, NB - 2)
            iteration(None, None, NB - 1)

        @block.sync
        def _(sp):
            def load(b):
                dveP.wait(sp, "xn1", b - 1)
                load_x.started(sp.dma_start(xin[:, :, :], x[b].rearrange("(t p) h -> p t h", p=P)))
                peA.wait(sp, "cT", b - 1)
                load_x.started(sp.dma_start(cin[:, :, :], ctx_in[b].rearrange("(t p) l -> p t l", p=P)))

            sp.dma_start(gates[0:1, 0:1], g_x.rearrange("(a n) -> a n", a=1)).then_inc(s_gates, 16)
            sp.dma_start(gates[0:1, 1:2], g_f.rearrange("(a n) -> a n", a=1)).then_inc(s_gates, 16)
            sp.dma_start(raw_kv, w_kv.rearrange("(m p) l -> p m l", p=P)).then_inc(s_raw[1], 16)
            sp.dma_start(raw_q, w_q.rearrange("(m p) h -> p m h", p=P)).then_inc(s_raw[0], 16)
            sp.dma_start(raw_o, w_out.rearrange("(m p) h -> p m h", p=P)).then_inc(s_raw[2], 16)
            load(0)

            def iteration(p, a, b):
                if a is not None:
                    Q5 = Q4[:, :, :].rearrange("p (g j) s -> p g j s", j=G)
                    K5 = K4[:, :, :].rearrange("p (g j) s -> p g j s", j=G)
                    peA.wait(sp, "ST7", a - 1)
                    actA.wait(sp, "k1", a)
                    dveA.wait(sp, "k1", a)
                    for r, part in enumerate((kh, kh, kl)):
                        for j in range(G):
                            stack_k.started(sp.dma_start(K5[HD * r:HD * r + HD, :, j, :], part[HD * j:HD * j + HD, :, :]))
                    stack_q.started(sp.dma_start(Q4[96:99, :, :], K4[99:102, :, :]))
                    actA.wait(sp, "q1", a)
                    apart(sp)
                    dveA.wait(sp, "q1", a)
                    for r, part in enumerate((qh, ql, qh)):
                        for j in range(G):
                            stack_q.started(sp.dma_start(Q5[HD * r:HD * r + HD, :, j, :], part[HD * j:HD * j + HD, :, :]))
                    dveA.wait(sp, "x1_1", a - 1)
                    load_res.started(sp.dma_start(xres[:, :, :], x[a].rearrange("(t p) h -> p t h", p=P)))
                if p is not None:
                    load(p)
                if a is not None:
                    actA.wait(sp, "mT", a)
                    for r in range(3):
                        for t in range(TT):
                            rows = mT[(r * TT + t) * NH:(r * TT + t + 1) * NH, :]
                            stack_m.started(sp.dma_start(Q4[96 + r:97 + r, :, t * P:(t + 1) * P], rows))
                if b is not None:
                    poolB.wait(sp, "o1", b)
                    store.started(sp.dma_start(out[b].rearrange("(t p) h -> p t h", p=P), ob[:, :, :]))

            iteration(1, 0, None)
            dveF.wait(sp, "q0", 0)
            sp.dma_start(raw_down.rearrange("p (m i) -> p m i", m=KT), w_down.rearrange("(m p) i -> p m i", p=P))\
                .then_inc(s_raw[5], 16)
            iteration(2, 1, 0)
            with sp.Fori(2, NB - 1) as i:
                iteration(i + 1, i, i - 1)
            iteration(None, NB - 1, NB - 2)
            iteration(None, None, NB - 1)
            store.wait(sp, NB - 1)

        @block.gpsimd
        def _(pool):
            n_const = [0]

            def const(instruction):
                instruction.then_inc(s_const, 1)
                n_const[0] += 1
                pool.wait_ge(s_const, n_const[0])

            const(pool.memset(ident[:, :], 0.0))
            const(pool.memset(identb[:, :], 0.0))
            const(pool.memset(causal4[:, :, :], 0.0))
            const(pool.memset(ones[:, :], 1.0))
            const(pool.memset(pick[:, :, :], 0.0))
            const(pool.memset(minus_half[:, :], -0.5))
            const(pool.memset(Q4[96:128, :, :], 0.0))
            const(pool.memset(K4[96:128, :, :], 0.0))
            const(pool.memset(K4[96:99, :, :], 1.0))
            for m in (ident, identb):
                const(pool.affine_select(out=m[:, :], in_=m[:, :], compare_op=ALU.not_equal, fill=1.0,
                                         base=0, pattern=[[-1, P]], channel_multiplier=1))
            const(pool.affine_select(out=causal4[:, :, :], in_=causal4[:, :, :], compare_op=ALU.is_ge, fill=MASKED,
                                     base=0, pattern=[[0, 4], [-1, P]], channel_multiplier=1))
            for g in range(KT):
                const(pool.memset(pick[:, g, :].rearrange("p (a b) -> p a b", b=4)[:, :, g:g + 1], 1.0))

            pool.dma_start(index[:, :], down_index.rearrange("(i p) -> p i", p=P), allow_slow_non_contiguous=True)\
                .then_inc(s_index, 16)
            pool.wait_ge(s_index, 16)
            peW.wait(pool, "a9", 0)
            for i in range(IT):
                pool.indirect_dma_start(
                    out=raw_gate[:, i * H:(i + 1) * H], out_offset=None, in_=w_gate[:, :],
                    in_offset=bass.IndirectOffsetOnAxis(ap=index[:, i:i + 1], axis=0)).then_inc(s_raw[3], 16)

            def iteration(p, a, b):
                if b is not None:
                    dveB.wait(pool, "ag1", b)
                    apart(pool)
                    poolB.done(pool.tensor_scalar(var_eps2[:, :], mv2[:, :, 1], LN_EPS, None, ALU.add), "ve")
                    poolB.wait(pool, "ve", b)
                    poolB.done(pool.tensor_tensor(rstd2[:, :], var_eps2[:, :], minus_half[:, :], ALU.pow), "rs")
                if a is not None:
                    for c in range(NC):
                        actA.wait(pool, f"e{c}", a)
                        apart(pool)
                        for h, view in (("a", PT[:, c, 0:512].rearrange("p (h s) -> p h s", s=S)[:, :, 0:P]),
                                        ("b", PT[:, c, 512:768].rearrange("p (h s) -> p h s", s=P))):
                            poolA.done(pool.affine_select(out=view, in_=view, compare_op=ALU.is_ge, fill=0.0, base=0,
                                                          pattern=[[0, 2], [1, P]], channel_multiplier=-1), f"sel{c}{h}")
                if p is not None:
                    pool_ln(p)
                if b is not None:
                    store.wait(pool, b - 1)
                    for t in range(TT):
                        dveB.wait(pool, f"y{t}", b)
                        poolB.done(pool.tensor_tensor(ob[:, t, :], yb[:, t, :], x1[:, t, :], ALU.add), f"o{t}")

            def pool_ln(p):
                dveP.wait(pool, "ag1", p)
                apart(pool)
                poolP.done(pool.tensor_scalar(var_eps[:, :], mv[:, :, 1], LN_EPS, None, ALU.add), "ve")
                poolP.wait(pool, "ve", p)
                poolP.done(pool.tensor_tensor(rstd[:, :], var_eps[:, :], minus_half[:, :], ALU.pow), "rs")

            pool_ln(0)
            iteration(1, 0, None)
            peA.wait(pool, "sum", 0)
            for i in range(IT):
                pool.indirect_dma_start(
                    out=raw_up[:, i * H:(i + 1) * H], out_offset=None, in_=w_up[:, :],
                    in_offset=bass.IndirectOffsetOnAxis(ap=index[:, i:i + 1], axis=0)).then_inc(s_raw[4], 16)
            iteration(2, 1, 0)
            with pool.Fori(2, NB - 1) as i:
                iteration(i + 1, i, i - 1)
            iteration(None, NB - 1, NB - 2)
            iteration(None, None, NB - 1)

        ring = [wk[0], wk[1], ff[0], ff[1]]
        w_parts = [(WkvTh[:, 512 * j:512 * j + 512], WkvTl[:, 512 * j:512 * j + 512]) for j in range(2)]
        w_parts += [(WqTh[:, k, :], WqTl[:, k, :]) for k in range(KT)]
        w_parts += [(WoTh[:, k, :], WoTl[:, k, :]) for k in range(KT)]

        def mlp_weights():
            for j in range(3):
                for i in range(0, IT, 2):
                    yield j, i, min(2, IT - i)

        @block.tensor
        def _(pe):
            pe.wait_ge(s_const, N_CONST)
            pe.wait_ge(s_gates, 32)
            peW.done(pe.matmul(att[0][:, 0:2], ones[0:1, :], gates[0:1, :], start=True, stop=True), "g")
            for n in range(10):
                if n in (0, 2, 6):
                    pe.wait_ge(s_raw[{0: 1, 2: 0, 6: 2}[n]], 16)
                if n >= 4:
                    dveW.wait(pe, f"a{n - 4}", 0)
                for m in range(4):
                    src = raw_kv[:, 4 * n + m, :] if n < 2 else (raw_q if n < 6 else raw_o)[:, m, (n - 2) % 4 * P:(n - 2) % 4 * P + P]
                    last = pe.transpose(ring[n % 4][:, m * P:(m + 1) * P], src, ident[:, :])
                peW.done(last, f"a{n}")

            def products(out_ap, terms):
                for n, (lhs, rhs) in enumerate(terms):
                    last = pe.matmul(out_ap, lhs, rhs, start=(n == 0), stop=(n == len(terms) - 1))
                return last

            def project(b):
                dveP.wait(pe, "xn1", b)
                for j in range(2):
                    w = wkb(f"xT{j}", pe, b)
                    for kk in range(2):
                        for t in range(TT):
                            last = pe.transpose(w[:, kk * S + t * P:kk * S + t * P + P],
                                                xn[:, t, (2 * j + kk) * P:(2 * j + kk + 1) * P], ident[:, :])
                    peA.done(last, f"xT{j}")
                load_x.wait(pe, b)
                w = wkb("cT", pe, b)
                for t in range(TT):
                    last = pe.transpose(w[:, t * P:(t + 1) * P], cin[:, t, :], ident[:, :])
                peA.done(last, "cT")
                actA.wait(pe, "cT", b)
                dveA.wait(pe, "cT", b)
                for j in range(2):
                    w = wkb(f"k{j}", pe, b)
                    for mm in range(2):
                        m = slice((2 * j + mm) * P, (2 * j + mm + 1) * P)
                        last = products(w[:, mm * S:(mm + 1) * S],
                                        [(WkvTh[:, m], cTh[:, :]), (WkvTh[:, m], cTl[:, :]), (WkvTl[:, m], cTh[:, :])])
                    peA.done(last, f"k{j}")
                for t in range(TT):
                    w = wkb(f"v{t}", pe, b)
                    tok = slice(t * P, (t + 1) * P)
                    peA.done(products(w[:, :], [(cTh[:, tok], WkvTh[:, H:]), (cTh[:, tok], WkvTl[:, H:]),
                                                (cTl[:, tok], WkvTh[:, H:])]), f"v{t}")
                actA.wait(pe, "xT1", b)
                dveA.wait(pe, "xT1", b)
                for j in range(2):
                    w = wkb(f"q{j}", pe, b)
                    for mm in range(2):
                        m = slice((2 * j + mm) * P, (2 * j + mm + 1) * P)
                        last = products(w[:, mm * S:(mm + 1) * S],
                                        [(a[:, k, m], c[:, k, :]) for k in range(KT)
                                         for a, c in ((WqTh, xTh), (WqTh, xTl), (WqTl, xTh))])
                    peA.done(last, f"q{j}")

            def scores(b, c):
                if c == 0:
                    stack_k.wait(pe, b)
                    stack_q.wait(pe, b)
                if c >= 2:
                    dveA.wait(pe, f"mx{c - 2}b", b)
                else:
                    actA.wait(pe, f"e{NC - 2 + c}", b - 1)
                w = att[c % 2]
                pe.matmul(w[:, 0:512], identb[:, :], causal4[:, :, :].rearrange("p a k -> p (a k)"),
                          start=True, stop=False, skip_group_check=True)
                for h in range(2):
                    q0, q1 = Q4[:, 2 * c + h, 0:P], Q4[:, 2 * c + h, P:S]
                    k0, k1 = K4[:, 2 * c + h, 0:P], K4[:, 2 * c + h, P:S]
                    pe.matmul(w[:, h * P:(h + 1) * P], q0, k0, start=False, stop=True, skip_group_check=True)
                    pe.matmul(w[:, (2 + h) * P:(3 + h) * P], q1, k1, start=False, stop=True, skip_group_check=True)
                    last = pe.matmul(w[:, (4 + h) * P:(5 + h) * P], q1, k0, start=True, stop=True)
                peA.done(last, f"S{c}")

            def shifted(b, c):
                if c == 0:
                    stack_m.wait(pe, b)
                if c >= 2:
                    actA.wait(pe, f"e{c - 2}", b)
                else:
                    dveA.wait(pe, f"mx{NC - 2 + c}b", b)
                w = att[c % 2]
                for h in range(2):
                    head = 2 * c + h
                    pe.matmul(w[:, h * S:(h + 1) * S], K4[:, head, 0:P], Q4[:, head, :], start=True, stop=True)
                    last = pe.matmul(w[:, (4 + h) * P:(5 + h) * P], K4[:, head, P:S], Q4[:, head, P:S], start=True, stop=True)
                peA.done(last, f"ST{c}")

            def weighted(b, g):
                w = wkb(f"PV{g}", pe, b)
                if g == 0:
                    actA.wait(pe, "v1", b)
                poolA.wait(pe, f"sel{2 * g + 1}b", b)
                for t in range(TT):
                    for j in range(G):
                        c, h = 2 * g + j // 2, j % 2
                        p = PT[:, c, h * S:(h + 1) * S] if t == 0 else PT[:, c, (4 + h) * P:(5 + h) * P]
                        last = pe.matmul(w[HD * j:HD * j + HD, t * P:S], V[:, t, (G * g + j) * HD:(G * g + j + 1) * HD], p,
                                         start=(t == 0), stop=(t == TT - 1), skip_group_check=True)
                peA.done(last, f"PV{g}")

            def sums(b):
                w = wkb("sum", pe, b)
                for g in range(KT):
                    for t in range(TT):
                        for j in range(G):
                            c, h = 2 * g + j // 2, j % 2
                            p = PT[:, c, h * S:(h + 1) * S] if t == 0 else PT[:, c, (4 + h) * P:(5 + h) * P]
                            last = pe.matmul(w[HD * j:HD * j + HD, t * P:S], pick[:, g, :], p, start=(g == 0 and t == 0),
                                             stop=(g == KT - 1 and t == TT - 1), skip_group_check=True)
                peA.done(last, "sum")

            def projected(b, t):
                if t == 0:
                    actA.wait(pe, "oh", b)
                    dveA.wait(pe, "ol", b)
                w = wkb(f"wo{t}", pe, b)
                tok = slice(t * P, (t + 1) * P)
                peA.done(products(w[:, :], [(a[:, g, tok], c[:, g, :]) for g in range(KT)
                                            for a, c in ((oh, WoTh), (oh, WoTl), (ol, WoTh))]), f"wo{t}")

            def mlp_in(b):
                dveB.wait(pe, "q", b)
                w = ffb("qxT", pe, b)[:, :].bitcast(BF16)
                for k in range(KT):
                    for t in range(TT):
                        last = pe.transpose(w[:, k * S + t * P:k * S + t * P + P], qx[:, t, k * P:(k + 1) * P], identb[:, :])
                peB.done(last, "qxT")
                dveB.wait(pe, "sp1", b)
                w = ffb("sxb", pe, b)
                for t in range(TT):
                    last = pe.matmul(w[:, t * P:(t + 1) * P], spread[:, t, :], ident[:, :], start=True, stop=True)
                peB.done(last, "sxb")

            def gate_up(b, n):
                if n == 0:
                    actB.wait(pe, "qxT", b)
                w = ffb(f"gu{n}", pe, b)
                i = slice(n * P, (n + 1) * P)
                products(w[:, 0:S], [(WgT[:, k, i], qxT[:, k, :]) for k in range(KT)])
                peB.done(products(w[:, S:], [(WuT[:, k, i], qxT[:, k, :]) for k in range(KT)]), f"gu{n}")

            def row_max(b):
                dveB.wait(pe, "ac1", b)
                w = ffb("amT", pe, b)
                for t in range(TT):
                    for n in range(2):
                        last = pe.transpose(w[:, (2 * t + n) * P:(2 * t + n + 1) * P], tmax[:, n, t * P:(t + 1) * P],
                                            ident[:, :])
                peB.done(last, "amT")

            def row_inv(b):
                dveB.wait(pe, "sq1", b)
                w = ffb("invb", pe, b)
                for t in range(TT):
                    last = pe.matmul(w[:, t * P:(t + 1) * P], spread2[:, t, :], ident[:, :], start=True, stop=True)
                peB.done(last, "invb")

            def down(b, t):
                if t == 0:
                    dveB.wait(pe, "Q", b)
                w = ffb(f"dn{t}", pe, b)
                peB.done(products(w[:, :], [(dq[:, 1, i, t * P:(t + 1) * P], WdT[:, i, :]) for i in range(IT)]), f"dn{t}")

            def iteration(p, a, b):
                if a is not None:
                    project(a)
                if b is not None:
                    mlp_in(b)
                for n in range(IT):
                    if b is not None:
                        gate_up(b, n)
                    if a is not None and n >= 3:
                        scores(a, n - 3)
                if a is not None:
                    dveA.wait(pe, "m3", a)
                    w = wkb("mT", pe, a)[0:3 * TT * NH, 0:P // 2].bitcast(BF16)
                    peA.done(pe.transpose(w, m_parts[:, :, :].rearrange("p r n -> p (r n)"), identb[:, :]), "mT")
                if b is not None:
                    row_max(b)
                for c in range(NC):
                    if a is not None:
                        shifted(a, c)
                    if b is not None and c == 0:
                        row_inv(b)
                    if a is not None and c in (2, 4, 6):
                        weighted(a, c // 2 - 1)
                if a is not None:
                    weighted(a, KT - 1)
                    sums(a)
                if b is not None:
                    down(b, 0)
                    down(b, 1)
                if a is not None:
                    projected(a, 0)
                    projected(a, 1)

            iteration(1, 0, None)
            for n, (j, i, k) in enumerate(mlp_weights()):
                if i == 0:
                    dveF.wait(pe, f"q{j}", 0)
                if n >= 2:
                    actF.wait(pe, f"t{n - 2}", 0)
                w = ff[n % 2][:, :].bitcast(BF16)
                for u in range(k):
                    for m in range(KT):
                        if j < 2:
                            dst = w[:, m * k * P + u * P:m * k * P + u * P + P]
                            src = wq8[:, (i + u) * H + m * P:(i + u) * H + m * P + P]
                        else:
                            dst = w[:, u * H + m * P:u * H + m * P + P]
                            src = wq8[:, m * I + (i + u) * P:m * I + (i + u) * P + P]
                        last = pe.transpose(dst, src, identb[:, :])
                peF.done(last, f"t{n}")
            dveF.wait(pe, "spread", 0)
            actF.wait(pe, "t16", 0)
            for m in range(KT):
                last = pe.matmul(ff[0][:, m * P:(m + 1) * P], cx[:, 0, m * P:(m + 1) * P], ident[:, :], start=True, stop=True)
            peF.done(last, "sc")
            dveF.wait(pe, "dsc", 0)
            iteration(2, 1, 0)
            with pe.Fori(2, NB - 1) as i:
                iteration(i + 1, i, i - 1)
            iteration(None, NB - 1, NB - 2)
            iteration(None, None, NB - 1)

        @block.scalar
        def _(act):
            def copy(dst, src):
                return act.activation(dst, src, ACT.Copy)

            peW.wait(act, "g", 0)
            actW.done(act.activation(tanh_g[:, :], att[0][:, 0:2], ACT.Tanh), "tanh")
            for n in range(10):
                peW.wait(act, f"a{n}", 0)
                actW.done(copy(w_parts[n][0], ring[n % 4][:, :]), f"a{n}")

            def take(b, progress, pe_progress, use, w, dst, func=None):
                pe_progress.wait(act, use, b)
                progress.done(copy(dst, w), use)

            def lift(progress, dve_progress, ready, value, dst, step, b):
                dve_progress.wait(act, ready, b)
                progress.done(act.activation(dst[:, :, :] if len(dst.shape) == 3 else dst, value[:, :, :] if len(value.shape) == 3 else value,
                                             ACT.Abs, scale=ROUND_LIFT), step)

            def project(b):
                peA.wait(act, "q1", b - 1)
                for j in range(2):
                    take(b, actA, peA, f"xT{j}", wkb(f"xT{j}")[:, :], xTh[:, 2 * j:2 * j + 2, :].rearrange("p k s -> p (k s)"))
                take(b, actA, peA, "cT", wkb("cT")[:, 0:S], cTh[:, :])
                stack_k.wait(act, b - 1)
                for j in range(2):
                    take(b, actA, peA, f"k{j}", wkb(f"k{j}")[:, :], kh[:, 2 * j:2 * j + 2, :].rearrange("p k s -> p (k s)"))
                peA.wait(act, "PV3", b - 1)
                for t in range(TT):
                    take(b, actA, peA, f"v{t}", wkb(f"v{t}")[:, :], V[:, t, :])
                stack_q.wait(act, b - 1)
                for j in range(2):
                    take(b, actA, peA, f"q{j}", wkb(f"q{j}")[:, :], qh[:, 2 * j:2 * j + 2, :].rearrange("p k s -> p (k s)"))

            def exps(b, c):
                if c == 0:
                    peA.wait(act, "sum", b - 1)
                peA.wait(act, f"ST{c}", b)
                actA.done(act.activation(PT[:, c, :], att[c % 2][:, 0:768], ACT.Exp, scale=SCALE), f"e{c}")

            def take_o(b, g):
                if g == 0:
                    dveA.wait(act, "on", b - 1)
                peA.wait(act, f"PV{g}", b)
                actA.done(copy(O[:, g, :], wkb(f"PV{g}")[:, 0:S]), f"O{g}")

            def iteration(p, a, b):
                if a is not None:
                    project(a)
                if b is not None:
                    lift(actB, dveB, "x1", cx, dx, "absx", b)
                    peB.wait(act, f"gu{IT - 1}", b - 1)
                    take(b, actB, peB, "qxT", ffb("qxT")[:, :].bitcast(BF16), qxT[:, :, :].rearrange("p k s -> p (k s)"))
                    dveB.wait(act, f"gs{IT - 1}", b - 1)
                    take(b, actB, peB, "sxb", ffb("sxb")[:, 0:S], sxb[:, :])
                    for n in range(IT):
                        dveB.wait(act, f"gs{n}", b)
                        if n >= 2:
                            dveB.wait(act, f"t{n - 2}", b)
                        actB.done(act.activation(sl[:, n % 2, :], gs[:, n % 2, :], ACT.Silu), f"silu{n}")
                if a is not None:
                    peA.wait(act, "mT", a)
                    stack_m.wait(act, a - 1)
                    actA.done(copy(mT[:, :], wkb("mT")[0:3 * TT * NH, 0:P // 2].bitcast(BF16)), "mT")
                    exps(a, 0)
                if b is not None:
                    dveB.wait(act, "X", b - 1)
                    take(b, actB, peB, "invb", ffb("invb")[:, 0:S], tinvb[:, :])
                    lift(actB, dveB, "X", T, dq[:, 0, :, :], "absT", b)
                if a is not None:
                    for c in range(1, NC):
                        exps(a, c)
                        if c in (2, 4, 6):
                            take_o(a, c // 2 - 1)
                    take_o(a, KT - 1)
                    dveA.wait(act, "on", a)
                    peA.wait(act, "wo1", a - 1)
                    actA.done(copy(oh[:, :, :], R[:, :, :]), "oh")

            iteration(1, 0, None)
            raws = (raw_gate, raw_up, raw_down)
            lift(actF, dveF, "x0", raws[0], wd, "abs0", 0)
            dveF.wait(act, "q0", 0)
            lift(actF, dveF, "x1", raws[1], wd, "abs1", 0)
            for n, (j, i, k) in enumerate(mlp_weights()):
                if n == 6:
                    dveF.wait(act, "q1", 0)
                    lift(actF, dveF, "x2", raws[2], wd, "abs2", 0)
                peF.wait(act, f"t{n}", 0)
                w = ff[n % 2][:, :].bitcast(BF16)
                if j < 2:
                    dst = (WgT, WuT)[j][:, :, i * P:(i + k) * P]
                    src = w[:, 0:KT * k * P].rearrange("p (m f) -> p m f", m=KT)
                else:
                    dst, src = WdT[:, i:i + k, :], w[:, 0:k * H].rearrange("p (u o) -> p u o", u=k)
                actF.done(copy(dst, src), f"t{n}")
            iteration(2, 1, 0)
            with act.Fori(2, NB - 1) as i:
                iteration(i + 1, i, i - 1)
            iteration(None, NB - 1, NB - 2)
            iteration(None, None, NB - 1)

        @block.vector
        def _(dve):
            def low(dst, w, high):
                return dve.tensor_tensor(dst, w, high, ALU.subtract)

            for n in range(10):
                actW.wait(dve, f"a{n}", 0)
                dveW.done(low(w_parts[n][1], ring[n % 4][:, :], w_parts[n][0]), f"a{n}")

            def to_fp8(progress, b, value, lift, dst, steps, lifted):
                lifted(dve, b)
                progress.done(dve.tensor_scalar(lift, lift, ROUND_FLOOR * ROUND_LIFT, None, ALU.max), steps[1])
                progress.wait(dve, steps[1], b)
                progress.done(dve.tensor_tensor(value, value, lift, ALU.add), steps[2])
                progress.wait(dve, steps[2], b)
                progress.done(dve.tensor_tensor(dst, value, lift, ALU.subtract), steps[3])

            def mlp_matrix(j, raw, rows):
                n = (IT * H) // rows
                dve.wait_ge(s_raw[3 + j], 16 * (1 if j == 2 else IT))
                r = raw.rearrange("p (n f) -> p n f", n=n)
                dveF.done(dve.tensor_reduce(wmax[:, j, 0:n], r, AX.X, ALU.max, apply_absolute_value=True), f"mx{j}")
                dveF.wait(dve, f"mx{j}", 0)
                dveF.done(dve.reciprocal(winv[:, j, 0:n], wmax[:, j, 0:n]), f"rc{j}")
                dveF.wait(dve, f"rc{j}", 0)
                dveF.done(dve.tensor_scalar(winv[:, j, 0:n], winv[:, j, 0:n], FP8_MAX, None, ALU.mult), f"iv{j}")
                dveF.done(dve.tensor_scalar(wscale[:, j, 0:n], wmax[:, j, 0:n], 1.0 / FP8_MAX, None, ALU.mult), f"sc{j}")
                dveF.wait(dve, f"iv{j}", 0)
                for m in range(n):
                    last = dve.tensor_scalar(r[:, m, :], r[:, m, :], winv[:, j, m:m + 1], None, ALU.mult)
                dveF.done(last, f"x{j}")
                if j:
                    peF.wait(dve, f"t{6 * j - 1}", 0)
                to_fp8(dveF, 0, raw, wd, wq8, [f"x{j}", f"d{j}", f"y{j}", f"q{j}"],
                       lambda eng, b: actF.wait(eng, f"abs{j}", b))

            def layer_norm(b):
                load_x.wait(dve, b)
                for t in range(TT):
                    dveP.done(dve.bn_stats(bn[:, t, :], xin[:, t, :]), f"st{t}")
                for t in range(TT):
                    dveP.wait(dve, f"st{t}", b)
                    apart(dve)
                    dveP.done(dve.bn_aggr(mv[:, t, :], bn[:, t, :]), f"ag{t}")
                peA.wait(dve, "xT1", b - 1)
                poolP.wait(dve, "rs", b)
                for t in range(TT):
                    dveP.done(dve.tensor_scalar(xn[:, t, :], xin[:, t, :], mv[:, t, 0:1], rstd[:, t:t + 1],
                                                ALU.subtract, ALU.mult), f"xn{t}")

            def take_low(b, use, w, dst, high):
                actA.wait(dve, use, b)
                dveA.done(low(dst, w, high), use)

            def take2(b, use, dst, high):
                j = int(use[-1])
                take_low(b, use, wkb(use)[:, :], dst[:, 2 * j:2 * j + 2, :].rearrange("p k s -> p (k s)"),
                         high[:, 2 * j:2 * j + 2, :].rearrange("p k s -> p (k s)"))

            def maxima(b, c):
                peA.wait(dve, f"S{c}", b)
                w = att[c % 2]
                dveA.done(dve.tensor_reduce(mx[:, 0, 2 * c:2 * c + 2], w[:, 0:2 * P].rearrange("p (h k) -> p h k", h=2),
                                            AX.X, ALU.max), f"mx{c}a")
                dveA.done(dve.tensor_reduce(mx[:, 1, 2 * c:2 * c + 2],
                                            w[:, 2 * P:6 * P].rearrange("p (r h k) -> p h r k", r=2, h=2),
                                            AX.XY, ALU.max), f"mx{c}b")

            def max_parts(b):
                dveA.wait(dve, f"mx{NC - 1}b", b)
                m = mx[:, :, :].rearrange("p t h -> p (t h)")
                dveA.done(dve.tensor_scalar(m_parts[:, 0, :], m, -1.0, None, ALU.mult), "m1")
                dveA.wait(dve, "m1", b)
                dveA.done(dve.scalar_tensor_tensor(out=m_rest[:, 0, :], in0=m, scalar=-1.0, in1=m_parts[:, 0, :],
                                                   op0=ALU.mult, op1=ALU.subtract), "r1")
                dveA.wait(dve, "r1", b)
                dveA.done(dve.tensor_copy(m_parts[:, 1, :], m_rest[:, 0, :]), "m2")
                dveA.wait(dve, "m2", b)
                dveA.done(dve.tensor_tensor(m_parts[:, 2, :], m_rest[:, 0, :], m_parts[:, 1, :], ALU.subtract), "m3")

            def normalise(b):
                peA.wait(dve, "sum", b)
                dveA.done(dve.reciprocal(rsum[:, :], wkb("sum")[:, 0:S]), "rc")
                dveA.wait(dve, "rc", b)
                apart(dve)
                for g in range(KT):
                    dveA.done(dve.stream_shuffle(out=R[:, g, :], in_=rsum[:, :], mask=[g] * HD), f"sh{g}")
                actA.wait(dve, "O3", b)
                dveA.wait(dve, "sh3", b)
                dveA.done(dve.tensor_tensor(R[:, :, :], O[:, :, :], R[:, :, :], ALU.mult), "on")
                actA.wait(dve, "oh", b)
                dveA.done(low(ol[:, :, :], R[:, :, :], oh[:, :, :]), "ol")

            def residual(b):
                load_res.wait(dve, b)
                poolB.wait(dve, "o1", b - 1)
                for t in range(TT):
                    peA.wait(dve, f"wo{t}", b)
                    dveA.done(dve.scalar_tensor_tensor(out=x1[:, t, :], in0=wkb(f"wo{t}")[:, :], scalar=tanh_g[:, 0:1],
                                                       in1=xres[:, t, :], op0=ALU.mult, op1=ALU.add), f"x1_{t}")

            def norm2_stats(b):
                for t in range(TT):
                    dveA.wait(dve, f"x1_{t}", b)
                    dveB.done(dve.bn_stats(bn2[:, t, :], x1[:, t, :]), f"st{t}")
                for t in range(TT):
                    dveB.wait(dve, f"st{t}", b)
                    apart(dve)
                    dveB.done(dve.bn_aggr(mv2[:, t, :], bn2[:, t, :]), f"ag{t}")
                for t in range(TT):
                    dveB.wait(dve, f"ag{t}", b)
                    dveB.done(dve.tensor_scalar(cx[:, t, :], x1[:, t, :], mv2[:, t, 0:1], None, ALU.subtract), f"c{t}")

            def norm2_scales(b):
                dveB.wait(dve, "c1", b)
                dveB.done(dve.tensor_reduce(amax[:, :], cx[:, :, :], AX.X, ALU.max, apply_absolute_value=True), "am")
                poolB.wait(dve, "rs", b)
                dveB.wait(dve, "am", b)
                dveB.done(dve.tensor_tensor(sx[:, :], amax[:, :], rstd2[:, :], ALU.mult), "sx0")
                dveB.wait(dve, "sx0", b)
                dveB.done(dve.tensor_scalar(sx[:, :], sx[:, :], 1.0 / FP8_MAX, None, ALU.mult), "sx1")
                dveB.done(dve.reciprocal(ainv[:, :], amax[:, :]), "rc")
                dveB.wait(dve, "rc", b)
                dveB.done(dve.tensor_scalar(ainv[:, :], ainv[:, :], FP8_MAX, None, ALU.mult), "iv")
                dveB.wait(dve, "iv", b)
                for t in range(TT):
                    dveB.done(dve.tensor_scalar(cx[:, t, :], cx[:, t, :], ainv[:, t:t + 1], None, ALU.mult), f"x{t}")

            def norm2_fp8(b):
                peB.wait(dve, "qxT", b - 1)
                to_fp8(dveB, b, cx[:, :, :], dx[:, :, :], qx[:, :, :], ["x1", "d", "y", "q"],
                       lambda eng, b: actB.wait(eng, "absx", b))
                peB.wait(dve, "sxb", b - 1)
                for t in range(TT):
                    dveB.done(dve.tensor_scalar(spread[:, t, :], ones[:, :], sx[:, t:t + 1], None, ALU.mult), f"sp{t}")

            def gate(b, n):
                if n == 0:
                    actB.wait(dve, "sxb", b)
                peB.wait(dve, f"gu{n}", b)
                if n >= 2:
                    actB.wait(dve, f"silu{n - 2}", b)
                dveB.done(dve.scalar_tensor_tensor(out=gs[:, n % 2, :], in0=ffb(f"gu{n}")[:, 0:S], scalar=wscale[:, 0, n:n + 1],
                                                   in1=sxb[:, :], op0=ALU.mult, op1=ALU.mult), f"gs{n}")

            def up(b, n):
                if n == 0:
                    peB.wait(dve, "dn1", b - 1)
                actB.wait(dve, f"silu{n}", b)
                dveB.done(dve.scalar_tensor_tensor(out=T[:, n, :], in0=ffb(f"gu{n}")[:, S:], scalar=wscale[:, 1, n:n + 1],
                                                   in1=sl[:, n % 2, :], op0=ALU.mult, op1=ALU.mult), f"t{n}")

            def largest(b, n):
                first, last = ((0, 6), (6, IT))[n]
                dveB.wait(dve, f"t{last - 1}", b)
                if n == 0:
                    peB.wait(dve, "amT", b - 1)
                dveB.done(dve.tensor_reduce(tmax[:, n, :], T[:, first:last, :].rearrange("p i s -> p s i"), AX.X, ALU.max,
                                            apply_absolute_value=True), f"ac{n}")

            def mlp_scales(b):
                peB.wait(dve, "amT", b)
                dveB.done(dve.tensor_reduce(tm[:, :], ffb("amT")[:, :].rearrange("p (t i) -> p t i", t=TT), AX.X, ALU.max), "mt")
                dveB.wait(dve, "mt", b)
                dveB.done(dve.tensor_tensor(st[:, :], tm[:, :], sx[:, :], ALU.mult), "st_a")
                dveB.wait(dve, "st_a", b)
                dveB.done(dve.tensor_scalar(st[:, :], st[:, :], 1.0 / FP8_MAX, None, ALU.mult), "st_b")
                dveB.done(dve.reciprocal(tinv[:, :], tm[:, :]), "rc2")
                dveB.wait(dve, "rc2", b)
                dveB.done(dve.tensor_scalar(tinv[:, :], tinv[:, :], FP8_MAX, None, ALU.mult), "iv2")
                dveB.wait(dve, "iv2", b)
                peB.wait(dve, "invb", b - 1)
                for t in range(TT):
                    dveB.done(dve.tensor_scalar(spread2[:, t, :], ones[:, :], tinv[:, t:t + 1], None, ALU.mult), f"sq{t}")

            def mlp_fp8(b):
                actB.wait(dve, "invb", b)
                dveB.wait(dve, "ac1", b)
                dveB.done(dve.tensor_tensor(T[:, :, :], T[:, :, :], tinvb[:, :].unsqueeze(1).to_broadcast([P, IT, S]),
                                            ALU.mult), "X")
                flat = lambda ap: ap.rearrange("p i s -> p (i s)")
                to_fp8(dveB, b, flat(T[:, :, :]), flat(dq[:, 0, :, :]), flat(dq[:, 1, :, :]), ["X", "D", "Y", "Q"],
                       lambda eng, b: actB.wait(eng, "absT", b))

            def mlp_out(b, t):
                peB.wait(dve, f"dn{t}", b)
                poolB.wait(dve, f"o{t}", b - 1)
                dveB.done(dve.scalar_tensor_tensor(out=yb[:, t, :], in0=ffb(f"dn{t}")[:, :], scalar=st[:, t:t + 1],
                                                   in1=down_scale[:, :], op0=ALU.mult, op1=ALU.mult), f"y{t}")

            def iteration(p, a, b):
                if a is not None:
                    peA.wait(dve, "q1", a - 1)
                    take2(a, "xT0", xTl, xTh)
                    take2(a, "xT1", xTl, xTh)
                if b is not None:
                    norm2_stats(b)
                if a is not None:
                    take_low(a, "cT", wkb("cT")[:, 0:S], cTl[:, :], cTh[:, :])
                    stack_k.wait(dve, a - 1)
                    take2(a, "k0", kl, kh)
                    take2(a, "k1", kl, kh)
                if b is not None:
                    norm2_scales(b)
                if a is not None:
                    stack_q.wait(dve, a - 1)
                    take2(a, "q0", ql, qh)
                    take2(a, "q1", ql, qh)
                if b is not None:
                    norm2_fp8(b)
                for n in range(IT + 2):
                    if b is not None:
                        for step, m in mlp_order(IT, n):
                            {"gs": gate, "t": up, "ac": largest}[step](b, m)
                    if a is not None and 3 <= n < 3 + NC:
                        maxima(a, n - 3)
                if a is not None:
                    max_parts(a)
                if b is not None:
                    mlp_scales(b)
                    mlp_fp8(b)
                if a is not None:
                    normalise(a)
                if p is not None:
                    layer_norm(p)
                if b is not None:
                    mlp_out(b, 0)
                    mlp_out(b, 1)
                if a is not None:
                    residual(a)

            dve.wait_ge(s_const, N_CONST)
            layer_norm(0)
            iteration(1, 0, None)
            mlp_matrix(0, raw_gate, H)
            mlp_matrix(1, raw_up, H)
            mlp_matrix(2, raw_down, I)
            dveF.wait(dve, "q2", 0)
            for m in range(KT):
                last = dve.tensor_scalar(cx[:, 0, m * P:(m + 1) * P], ones[:, :], wscale[:, 2, m:m + 1], None, ALU.mult)
            dveF.done(last, "spread")
            peF.wait(dve, "sc", 0)
            actW.wait(dve, "tanh", 0)
            dveF.done(dve.tensor_scalar(down_scale[:, :], ff[0][:, :], tanh_g[:, 1:2], None, ALU.mult), "dsc")
            dveF.wait(dve, "dsc", 0)
            iteration(2, 1, 0)
            with dve.Fori(2, NB - 1) as i:
                iteration(i + 1, i, i - 1)
            iteration(None, NB - 1, NB - 2)
            iteration(None, None, NB - 1)


def mlp_order(n_tiles, n):
    halves = {7: 0, n_tiles + 1: 1}
    return ([(s, m) for s, m in (("gs", n), ("t", n - 1)) if 0 <= m < n_tiles]
            + ([("ac", halves[n])] if n in halves else []))


def mlp_steps(n_tiles):
    return [f"{s}{m}" for n in range(n_tiles + 2) for s, m in mlp_order(n_tiles, n)]


_INS = ["x", "ctx_512", "g_xattn", "g_ffn", "L0_xattn_Wq", "L0_xattn_Wkv_expand", "L0_xattn_Wout",
        "L0_ffn_w_gate", "L0_ffn_w_up", "L0_ffn_w_down", "L0_ffn_down_reorder_index"]


def kernel(**inputs):
    import numpy as _np
    import concourse.bacc as _bacc
    from concourse import mybir as _mybir
    from concourse.bass_utils import run_bass_kernel_spmd as _run

    nc = _bacc.Bacc("TRN2", target_bir_lowering=False, num_devices=1)
    arrays, args = {}, []
    for name in _INS:
        a = _np.ascontiguousarray(inputs[name])
        arrays[f"in_{name}_dram"] = a
        args.append(nc.dram_tensor(f"in_{name}_dram", a.shape, _mybir.dt.from_np(a.dtype), kind="ExternalInput").ap())
    args.append(nc.dram_tensor("out_0_dram", inputs["x"].shape, F32, kind="ExternalOutput").ap())
    gated_block_kernel(nc, *args)
    r = _run(nc, [arrays], core_ids=[0])
    return r.results[0]["out_0_dram"]
```

```python
from contextlib import ExitStack

import concourse.bass as bass
from concourse import mybir

P = 128
FP8_MAX = 448.0
ROUND_FLOOR = 1.5 * 2.0**-6
ROUND_LIFT = 2.0**20
LN_EPS = 1e-5
MASKED = -3.3e38

F32 = mybir.dt.float32
BF16 = mybir.dt.bfloat16
ALU = mybir.AluOpType
ACT = mybir.ActivationFunctionType
AX = mybir.AxisListType


class Progress:

    def __init__(self, sem, steps):
        self.sem = sem
        self.steps = list(steps)
        self.at = 0

    def done(self, instruction, step):
        assert self.steps[self.at % len(self.steps)] == step, (step, self.steps[self.at % len(self.steps)])
        self.at += 1
        instruction.then_inc(self.sem, 1)

    def wait(self, eng, step, b):
        value = b * len(self.steps) + self.steps.index(step) + 1
        if isinstance(value, int) and value <= 0:
            return
        eng.wait_ge(self.sem, value)


class Loads:

    def __init__(self, sem, n):
        self.sem = sem
        self.n = n

    def started(self, dma):
        dma.then_inc(self.sem, 16)

    def wait(self, eng, b):
        value = (b + 1) * (16 * self.n)
        if isinstance(value, int) and value <= 0:
            return
        eng.wait_ge(self.sem, value)


def names(prefix, n):
    return [f"{prefix}{i}" for i in range(n)]


def gated_block_kernel(nc, x, ctx_in, g_x, g_f, w_q, w_kv, w_out, w_gate, w_up, w_down, down_index, out):
    NB, S, H = x.shape
    L = ctx_in.shape[2]
    I = w_gate.shape[0]
    HD = 32
    NH = H // HD
    TT = S // P
    KT = H // P
    IT = I // P
    G = P // HD
    NC = NH // 2
    SCALE = float(HD) ** -0.5
    assert (TT, L, KT * P, IT * P) == (2, P, H, I) and KT == 4 and G == 4

    with ExitStack() as stack:
        def sb(name, shape, dt=F32):
            return stack.enter_context(nc.sbuf_tensor(name, shape, dt))

        def sem(name):
            return stack.enter_context(nc.semaphore(name))

        att = [stack.enter_context(nc.psum_tensor(f"att{i}", [P, 1024], F32)) for i in range(2)]
        wk = [stack.enter_context(nc.psum_tensor(f"wk{i}", [P, 512], F32)) for i in range(2)]
        ff = [stack.enter_context(nc.psum_tensor(f"ff{i}", [P, 512], F32)) for i in range(2)]

        ident = sb("ident", [P, P])
        identb = sb("identb", [P, P], BF16)
        ones = sb("ones", [P, P])
        causal4 = sb("causal4", [P, 4, P], BF16)
        pick = sb("pick", [P, KT, HD])
        minus_half = sb("minus_half", [P, TT])
        gates = sb("gates", [1, 2])
        tanh_g = sb("tanh_g", [P, 2])
        index = sb("index", [P, IT], mybir.dt.int32)

        WqTh = sb("WqTh", [P, KT, H], BF16)
        WqTl = sb("WqTl", [P, KT, H], BF16)
        WkvTh = sb("WkvTh", [P, 2 * H], BF16)
        WkvTl = sb("WkvTl", [P, 2 * H], BF16)
        WoTh = sb("WoTh", [P, KT, H], BF16)
        WoTl = sb("WoTl", [P, KT, H], BF16)
        WgT = sb("WgT", [P, KT, I], BF16)
        WuT = sb("WuT", [P, KT, I], BF16)
        WdT = sb("WdT", [P, IT, H], BF16)
        wscale = sb("wscale", [P, 3, IT])
        wmax = sb("wmax", [P, 3, IT])
        winv = sb("winv", [P, 3, IT])
        down_scale = sb("down_scale", [P, H])

        xin = sb("xin", [P, TT, H])
        cin = sb("cin", [P, TT, L])
        xres = sb("xres", [P, TT, H])
        bn = sb("bn", [P, TT, 6])
        mv = sb("mv", [P, TT, 2])
        var_eps = sb("var_eps", [P, TT])
        rstd = sb("rstd", [P, TT])
        xn = sb("xn", [P, TT, H])
        xTh = sb("xTh", [P, KT, S], BF16)
        xTl = sb("xTl", [P, KT, S], BF16)
        cTh = sb("cTh", [P, S], BF16)
        cTl = sb("cTl", [P, S], BF16)
        kh = sb("kh", [P, KT, S], BF16)
        kl = sb("kl", [P, KT, S], BF16)
        qh = sb("qh", [P, KT, S], BF16)
        ql = sb("ql", [P, KT, S], BF16)
        V = sb("V", [P, TT, H])
        Q4 = sb("Q4", [P, NH, S], BF16)
        K4 = sb("K4", [P, NH, S], BF16)
        mx = sb("mx", [P, NH, TT])
        m_parts = sb("m_parts", [P, 3, TT * NH], BF16)
        m_rest = sb("m_rest", [P, 2, TT * NH])
        mT = sb("mT", [3 * TT * NH, P], BF16)
        PT = sb("PT", [P, NC, 768])
        O = sb("O", [P, KT, S])
        rsum = sb("rsum", [P, S])
        R = sb("R", [P, KT, S])
        oh = sb("oh", [P, KT, S], BF16)
        ol = sb("ol", [P, KT, S], BF16)
        x1 = sb("x1", [P, TT, H])
        bn2 = sb("bn2", [P, TT, 6])
        mv2 = sb("mv2", [P, TT, 2])
        var_eps2 = sb("var_eps2", [P, TT])
        rstd2 = sb("rstd2", [P, TT])
        amax = sb("amax", [P, TT])
        ainv = sb("ainv", [P, TT])
        sx = sb("sx", [P, TT])
        T = sb("T", [P, IT, S])
        dq = sb("dq", [P, 2, IT, S], BF16)
        tmax = sb("tmax", [P, 2, S])
        tm = sb("tm", [P, TT])
        tinv = sb("tinv", [P, TT])
        st = sb("st", [P, TT])
        ob = sb("ob", [P, TT, H])

        raw_a = sb("raw_a", [P, IT * H])
        carved = [0]

        def carve(a, n, dt=F32):
            words = a * n * (2 if dt == BF16 else 4) // 4
            at, carved[0] = carved[0], carved[0] + words
            part = raw_a[:, at:at + words]
            part = part.bitcast(dt) if dt == BF16 else part
            return part.rearrange("p (a n) -> p a n", a=a)

        cx = carve(TT, H)
        dx = carve(TT, H, BF16)
        qx = carve(TT, H, BF16)
        qxT = carve(KT, S, BF16)
        gs = carve(2, S)
        sl = carve(2, S)
        yb = carve(TT, H)
        spread = carve(TT, P)
        spread2 = carve(TT, P)
        sxb = raw_a[:, carved[0]:carved[0] + S]
        tinvb = raw_a[:, carved[0] + S:carved[0] + 2 * S]
        assert carved[0] + 2 * S <= IT * H
        raw_q = PT[:, :, :].rearrange("p c n -> p (c n)")[:, 0:KT * H].rearrange("p (m h) -> p m h", m=KT)
        raw_kv = xn[:, :, :].rearrange("p t h -> p (t h)").rearrange("p (m l) -> p m l", l=L)
        raw_o = raw_a[:, 0:KT * H].rearrange("p (m h) -> p m h", m=KT)
        raw_gate = raw_a[:, :]
        raw_up = PT[:, :, :].rearrange("p c n -> p (c n)")[:, 0:IT * H]
        raw_down = raw_a[:, :]
        wd = T[:, :, :].bitcast(BF16).rearrange("p i s -> p (i s)")
        wq8 = dq[:, :, :, :].rearrange("p a i s -> p (a i s)")

        s_const = sem("s_const")
        s_index = sem("s_index")
        s_apart = sem("s_apart")
        s_gates = sem("s_gates")
        s_raw = [sem(f"s_raw_{n}") for n in ("q", "kv", "o", "gate", "up", "down")]
        peW = Progress(sem("peW"), ["g"] + names("a", 10))
        actW = Progress(sem("actW"), ["tanh"] + names("a", 10))
        dveW = Progress(sem("dveW"), names("a", 10))
        w_steps = [s + str(j) for j in range(3) for s in ("mx", "rc", "iv", "sc", "x", "d", "y", "q")]
        dveF = Progress(sem("dveF"), w_steps + ["spread", "dsc"])
        peF = Progress(sem("peF"), names("t", 18) + ["sc"])
        actF = Progress(sem("actF"), ["abs0", "abs1"] + names("t", 6) + ["abs2"] + [f"t{n}" for n in range(6, 18)])

        load_x = Loads(sem("load_x"), 2)
        load_res = Loads(sem("load_res"), 1)
        stack_k = Loads(sem("stack_k"), 12)
        stack_q = Loads(sem("stack_q"), 13)
        stack_m = Loads(sem("stack_m"), 1)
        store = Loads(sem("store"), 1)

        proj = ["xT0", "xT1", "cT", "k0", "k1", "q0", "q1"]
        peP = Progress(sem("peP"), proj + ["v0", "v1"])
        peA = Progress(sem("peA"), names("S", NC) + ["mT", "ST0", "ST1", "ST2", "ST3", "PV0", "ST4", "ST5", "PV1",
                                                     "ST6", "ST7", "PV2", "PV3", "sum", "wo0", "wo1"])
        peB = Progress(sem("peB"), ["qxT", "sxb"] + names("gu", IT) + ["amT", "invb", "dn0", "dn1"])
        dveL = Progress(sem("dveL"), ["st0", "st1", "ag0", "ag1", "xn0", "xn1"])
        dveP = Progress(sem("dveP"), proj)
        dveA = Progress(sem("dveA"), [f"mx{c}{h}" for c in range(NC) for h in "ab"]
                        + ["m1", "r1", "m2", "m3", "rc"] + names("sh", KT) + ["on", "ol", "x1_0", "x1_1"])
        dveB = Progress(sem("dveB"), ["st0", "st1", "ag0", "ag1", "c0", "c1", "am", "sx0", "sx1", "rc", "iv", "x0", "x1",
                                      "d", "y", "q", "sp0", "sp1"]
                        + mlp_steps(IT) + ["mt", "st_a", "st_b", "rc2", "iv2", "sq0", "sq1",
                                           "X0", "X1", "D0", "Y0", "Q0", "D1", "Y1", "Q1", "y0", "y1"])
        actP = Progress(sem("actP"), proj + ["v0", "v1"])
        actA = Progress(sem("actA"), ["mT", "e0", "e1", "e2", "e3", "O0", "e4", "e5", "O1", "e6", "e7", "O2", "O3", "oh"])
        actB = Progress(sem("actB"), ["absx", "qxT", "sxb"] + names("silu", IT) + ["invb", "absT0", "absT1"])
        poolL = Progress(sem("poolL"), ["ve", "rs"])
        poolA = Progress(sem("poolA"), [f"sel{c}{h}" for c in range(NC) for h in "ab"])
        poolB = Progress(sem("poolB"), ["ve", "rs", "o0", "o1"])

        wk_uses = proj + ["mT", "PV0", "PV1", "PV2", "PV3", "v0", "v1", "sum", "wo0", "wo1"]
        wk_freed = {n: (dveP, n) for n in proj}
        wk_freed |= {"v0": (actP, "v0"), "v1": (actP, "v1"), "mT": (actA, "mT"), "sum": (dveA, "rc")}
        wk_freed |= {f"PV{g}": (actA, f"O{g}") for g in range(KT)} | {f"wo{t}": (dveA, f"x1_{t}") for t in range(TT)}
        ff_uses = ["qxT", "sxb"] + names("gu", IT) + ["amT", "invb", "dn0", "dn1"]
        ff_freed = {"qxT": (actB, "qxT"), "sxb": (actB, "sxb"), "amT": (dveB, "mt"), "invb": (actB, "invb"),
                    "dn0": (dveB, "y0"), "dn1": (dveB, "y1")} | {f"gu{n}": (dveB, f"t{n}") for n in range(IT)}

        assert len(wk_uses) % 2 == 1 and len(ff_uses) % 2 == 1

        def bank(banks, uses, freed, use, eng=None, b=None):
            ahead = lambda u: 1 if u in proj or u in ("v0", "v1") else 0
            n = uses.index(use)
            if eng is not None:
                at = b - (ahead(use) if uses is wk_uses else 0)
                for m, lag in [(m, 0) for m in range(n - 2, -1, -2)] + \
                        [(m, lag) for lag in (1, 2) for m in range(len(uses) - 1 - n % 2, -1, -2)]:
                    batch = at - lag + (ahead(uses[m]) if uses is wk_uses else 0)
                    if not isinstance(batch, int) or 0 <= batch < NB:
                        progress, step = freed[uses[m]]
                        progress.wait(eng, step, batch)
                        break
            return banks[n % 2]

        def wkb(use, eng=None, b=None):
            return bank(wk, wk_uses, wk_freed, use, eng, b)

        def ffb(use, eng=None, b=None):
            return bank(ff, ff_uses, ff_freed, use, eng, b)

        N_CONST = 9 + 3 + KT

        def apart(eng):
            eng.sem_inc(s_apart, 1)

        block = stack.enter_context(nc.Block())

        def pipeline(eng, iteration, mlp_weights):
            iteration(1, 0, None, None)
            iteration(2, 1, 0, None)
            mlp_weights()
            iteration(3, 2, 1, 0)
            with eng.Fori(2, NB - 2) as i:
                iteration(i + 2, i + 1, i, i - 1)
            iteration(None, NB - 1, NB - 2, NB - 3)
            iteration(None, None, NB - 1, NB - 2)
            iteration(None, None, None, NB - 1)

        @block.sync
        def _(sp):
            def load_tokens(b):
                dveL.wait(sp, "xn1", b - 1)
                apart(sp)
                load_x.started(sp.dma_start(xin[:, :, :], x[b].rearrange("(t p) h -> p t h", p=P)))

            def load_context(b):
                peP.wait(sp, "cT", b - 1)
                apart(sp)
                load_x.started(sp.dma_start(cin[:, :, :], ctx_in[b].rearrange("(t p) l -> p t l", p=P)))

            sp.dma_start(gates[0:1, 0:1], g_x.rearrange("(a n) -> a n", a=1)).then_inc(s_gates, 16)
            sp.dma_start(gates[0:1, 1:2], g_f.rearrange("(a n) -> a n", a=1)).then_inc(s_gates, 16)
            sp.dma_start(raw_kv, w_kv.rearrange("(m p) l -> p m l", p=P)).then_inc(s_raw[1], 16)
            sp.dma_start(raw_q, w_q.rearrange("(m p) h -> p m h", p=P)).then_inc(s_raw[0], 16)
            sp.dma_start(raw_o, w_out.rearrange("(m p) h -> p m h", p=P)).then_inc(s_raw[2], 16)
            load_tokens(0)
            load_context(0)

            def iteration(l, p, a, b):
                if l is not None:
                    load_tokens(l)
                if a is not None:
                    dveA.wait(sp, "x1_1", a - 1)
                    apart(sp)
                    load_res.started(sp.dma_start(xres[:, :, :], x[a].rearrange("(t p) h -> p t h", p=P)))
                if l is not None:
                    load_context(l)
                if a is not None:
                    actA.wait(sp, "mT", a)
                    apart(sp)
                    stack_m.started(sp.dma_start(Q4[96:99, :, :].rearrange("r h (t s) -> r (h t) s", t=TT), mT[:, :]))
                if p is not None:
                    Q5 = Q4[:, :, :].rearrange("p (g j) s -> p g j s", j=G)
                    K5 = K4[:, :, :].rearrange("p (g j) s -> p g j s", j=G)
                    peA.wait(sp, "ST7", p - 1)
                    apart(sp)
                    actP.wait(sp, "k1", p)
                    apart(sp)
                    dveP.wait(sp, "k1", p)
                    apart(sp)
                    for r, part in enumerate((kh, kh, kl)):
                        for j in range(G):
                            stack_k.started(sp.dma_start(K5[HD * r:HD * r + HD, :, j, :], part[HD * j:HD * j + HD, :, :]))
                    stack_q.started(sp.dma_start(Q4[96:99, :, :], K4[99:102, :, :]))
                    actP.wait(sp, "q1", p)
                    apart(sp)
                    dveP.wait(sp, "q1", p)
                    apart(sp)
                    for r, part in enumerate((qh, ql, qh)):
                        for j in range(G):
                            stack_q.started(sp.dma_start(Q5[HD * r:HD * r + HD, :, j, :], part[HD * j:HD * j + HD, :, :]))
                if b is not None:
                    poolB.wait(sp, "o1", b)
                    apart(sp)
                    store.started(sp.dma_start(out[b].rearrange("(t p) h -> p t h", p=P), ob[:, :, :]))

            def mlp_weights():
                dveF.wait(sp, "q0", 0)
                sp.dma_start(raw_down.rearrange("p (m i) -> p m i", m=KT), w_down.rearrange("(m p) i -> p m i", p=P))\
                    .then_inc(s_raw[5], 16)

            pipeline(sp, iteration, mlp_weights)
            store.wait(sp, NB - 1)


        @block.gpsimd
        def _(pool):
            n_const = [0]

            def const(instruction):
                instruction.then_inc(s_const, 1)
                n_const[0] += 1
                pool.wait_ge(s_const, n_const[0])

            const(pool.memset(ident[:, :], 0.0))
            const(pool.memset(identb[:, :], 0.0))
            const(pool.memset(causal4[:, :, :], 0.0))
            const(pool.memset(ones[:, :], 1.0))
            const(pool.memset(pick[:, :, :], 0.0))
            const(pool.memset(minus_half[:, :], -0.5))
            const(pool.memset(Q4[96:128, :, :], 0.0))
            const(pool.memset(K4[96:128, :, :], 0.0))
            const(pool.memset(K4[96:99, :, :], 1.0))
            for m in (ident, identb):
                const(pool.affine_select(out=m[:, :], in_=m[:, :], compare_op=ALU.not_equal, fill=1.0,
                                         base=0, pattern=[[-1, P]], channel_multiplier=1))
            const(pool.affine_select(out=causal4[:, :, :], in_=causal4[:, :, :], compare_op=ALU.is_ge, fill=MASKED,
                                     base=0, pattern=[[0, 4], [-1, P]], channel_multiplier=1))
            for g in range(KT):
                const(pool.memset(pick[:, g, :].rearrange("p (a b) -> p a b", b=4)[:, :, g:g + 1], 1.0))

            pool.dma_start(index[:, :], down_index.rearrange("(i p) -> p i", p=P), allow_slow_non_contiguous=True)\
                .then_inc(s_index, 16)
            pool.wait_ge(s_index, 16)
            peW.wait(pool, "a9", 0)
            for i in range(IT):
                pool.indirect_dma_start(
                    out=raw_gate[:, i * H:(i + 1) * H], out_offset=None, in_=w_gate[:, :],
                    in_offset=bass.IndirectOffsetOnAxis(ap=index[:, i:i + 1], axis=0)).then_inc(s_raw[3], 16)

            def iteration(l, p, a, b):
                if b is not None:
                    dveB.wait(pool, "ag1", b)
                    apart(pool)
                    poolB.done(pool.tensor_scalar(var_eps2[:, :], mv2[:, :, 1], LN_EPS, None, ALU.add), "ve")
                    poolB.wait(pool, "ve", b)
                    poolB.done(pool.tensor_tensor(rstd2[:, :], var_eps2[:, :], minus_half[:, :], ALU.pow), "rs")
                if a is not None:
                    for c in range(NC):
                        actA.wait(pool, f"e{c}", a)
                        apart(pool)
                        for h, view in (("a", PT[:, c, 0:512].rearrange("p (h s) -> p h s", s=S)[:, :, 0:P]),
                                        ("b", PT[:, c, 512:768].rearrange("p (h s) -> p h s", s=P))):
                            poolA.done(pool.affine_select(out=view, in_=view, compare_op=ALU.is_ge, fill=0.0, base=0,
                                                          pattern=[[0, 2], [1, P]], channel_multiplier=-1), f"sel{c}{h}")
                if l is not None:
                    pool_ln(l)
                if b is not None:
                    store.wait(pool, b - 1)
                    for t in range(TT):
                        dveB.wait(pool, f"y{t}", b)
                        poolB.done(pool.tensor_tensor(ob[:, t, :], yb[:, t, :], x1[:, t, :], ALU.add), f"o{t}")

            def pool_ln(p):
                dveL.wait(pool, "ag1", p)
                apart(pool)
                poolL.done(pool.tensor_scalar(var_eps[:, :], mv[:, :, 1], LN_EPS, None, ALU.add), "ve")
                poolL.wait(pool, "ve", p)
                poolL.done(pool.tensor_tensor(rstd[:, :], var_eps[:, :], minus_half[:, :], ALU.pow), "rs")

            def mlp_weights():
                peA.wait(pool, "sum", 0)
                for i in range(IT):
                    pool.indirect_dma_start(
                        out=raw_up[:, i * H:(i + 1) * H], out_offset=None, in_=w_up[:, :],
                        in_offset=bass.IndirectOffsetOnAxis(ap=index[:, i:i + 1], axis=0)).then_inc(s_raw[4], 16)

            pool_ln(0)
            pipeline(pool, iteration, mlp_weights)

        ring = [wk[0], wk[1], ff[0], ff[1]]
        w_parts = [(WkvTh[:, 512 * j:512 * j + 512], WkvTl[:, 512 * j:512 * j + 512]) for j in range(2)]
        w_parts += [(WqTh[:, k, :], WqTl[:, k, :]) for k in range(KT)]
        w_parts += [(WoTh[:, k, :], WoTl[:, k, :]) for k in range(KT)]

        def mlp_tiles():
            for j in range(3):
                for i in range(0, IT, 2):
                    yield j, i, min(2, IT - i)

        @block.tensor
        def _(pe):
            pe.wait_ge(s_const, N_CONST)
            pe.wait_ge(s_gates, 32)
            peW.done(pe.matmul(att[0][:, 0:2], ones[0:1, :], gates[0:1, :], start=True, stop=True), "g")
            for n in range(10):
                if n in (0, 2, 6):
                    pe.wait_ge(s_raw[{0: 1, 2: 0, 6: 2}[n]], 16)
                if n >= 4:
                    dveW.wait(pe, f"a{n - 4}", 0)
                for m in range(4):
                    src = raw_kv[:, 4 * n + m, :] if n < 2 else (raw_q if n < 6 else raw_o)[:, m, (n - 2) % 4 * P:(n - 2) % 4 * P + P]
                    last = pe.transpose(ring[n % 4][:, m * P:(m + 1) * P], src, ident[:, :])
                peW.done(last, f"a{n}")

            def products(out_ap, terms):
                for n, (lhs, rhs) in enumerate(terms):
                    last = pe.matmul(out_ap, lhs, rhs, start=(n == 0), stop=(n == len(terms) - 1))
                return last

            def transposes(b):
                dveL.wait(pe, "xn1", b)
                for j in range(2):
                    w = wkb(f"xT{j}", pe, b)
                    for kk in range(2):
                        for t in range(TT):
                            last = pe.transpose(w[:, kk * S + t * P:kk * S + t * P + P],
                                                xn[:, t, (2 * j + kk) * P:(2 * j + kk + 1) * P], ident[:, :])
                    peP.done(last, f"xT{j}")
                load_x.wait(pe, b)
                w = wkb("cT", pe, b)
                for t in range(TT):
                    last = pe.transpose(w[:, t * P:(t + 1) * P], cin[:, t, :], ident[:, :])
                peP.done(last, "cT")

            def keys(b, j):
                if j == 0:
                    actP.wait(pe, "cT", b)
                    dveP.wait(pe, "cT", b)
                w = wkb(f"k{j}", pe, b)
                for mm in range(2):
                    m = slice((2 * j + mm) * P, (2 * j + mm + 1) * P)
                    last = products(w[:, mm * S:(mm + 1) * S],
                                    [(WkvTh[:, m], cTh[:, :]), (WkvTh[:, m], cTl[:, :]), (WkvTl[:, m], cTh[:, :])])
                peP.done(last, f"k{j}")

            def queries(b, j):
                if j == 0:
                    actP.wait(pe, "xT1", b)
                    dveP.wait(pe, "xT1", b)
                w = wkb(f"q{j}", pe, b)
                for mm in range(2):
                    m = slice((2 * j + mm) * P, (2 * j + mm + 1) * P)
                    last = products(w[:, mm * S:(mm + 1) * S],
                                    [(a[:, k, m], c[:, k, :]) for k in range(KT)
                                     for a, c in ((WqTh, xTh), (WqTh, xTl), (WqTl, xTh))])
                peP.done(last, f"q{j}")

            def values(b):
                for t in range(TT):
                    w = wkb(f"v{t}", pe, b)
                    tok = slice(t * P, (t + 1) * P)
                    peP.done(products(w[:, :], [(cTh[:, tok], WkvTh[:, H:]), (cTh[:, tok], WkvTl[:, H:]),
                                                (cTl[:, tok], WkvTh[:, H:])]), f"v{t}")

            def scores(b, c):
                if c == 0:
                    stack_k.wait(pe, b)
                    stack_q.wait(pe, b)
                if c >= 2:
                    dveA.wait(pe, f"mx{c - 2}b", b)
                else:
                    actA.wait(pe, f"e{NC - 2 + c}", b - 1)
                w = att[c % 2]
                pe.matmul(w[:, 0:512], identb[:, :], causal4[:, :, :].rearrange("p a k -> p (a k)"),
                          start=True, stop=False, skip_group_check=True)
                for h in range(2):
                    q0, q1 = Q4[:, 2 * c + h, 0:P], Q4[:, 2 * c + h, P:S]
                    k0, k1 = K4[:, 2 * c + h, 0:P], K4[:, 2 * c + h, P:S]
                    pe.matmul(w[:, h * P:(h + 1) * P], q0, k0, start=False, stop=True, skip_group_check=True)
                    pe.matmul(w[:, (2 + h) * P:(3 + h) * P], q1, k1, start=False, stop=True, skip_group_check=True)
                    last = pe.matmul(w[:, (4 + h) * P:(5 + h) * P], q1, k0, start=True, stop=True)
                peA.done(last, f"S{c}")

            def shifted(b, c):
                if c == 0:
                    stack_m.wait(pe, b)
                if c >= 2:
                    actA.wait(pe, f"e{c - 2}", b)
                else:
                    dveA.wait(pe, f"mx{NC - 2 + c}b", b)
                w = att[c % 2]
                for h in range(2):
                    head = 2 * c + h
                    pe.matmul(w[:, h * S:(h + 1) * S], K4[:, head, 0:P], Q4[:, head, :], start=True, stop=True)
                    last = pe.matmul(w[:, (4 + h) * P:(5 + h) * P], K4[:, head, P:S], Q4[:, head, P:S], start=True, stop=True)
                peA.done(last, f"ST{c}")

            def weighted(b, g):
                w = wkb(f"PV{g}", pe, b)
                if g == 0:
                    actP.wait(pe, "v1", b)
                poolA.wait(pe, f"sel{2 * g + 1}b", b)
                for t in range(TT):
                    for j in range(G):
                        c, h = 2 * g + j // 2, j % 2
                        p = PT[:, c, h * S:(h + 1) * S] if t == 0 else PT[:, c, (4 + h) * P:(5 + h) * P]
                        last = pe.matmul(w[HD * j:HD * j + HD, t * P:S], V[:, t, (G * g + j) * HD:(G * g + j + 1) * HD], p,
                                         start=(t == 0), stop=(t == TT - 1), skip_group_check=True)
                peA.done(last, f"PV{g}")

            def sums(b):
                w = wkb("sum", pe, b)
                for g in range(KT):
                    for t in range(TT):
                        for j in range(G):
                            c, h = 2 * g + j // 2, j % 2
                            p = PT[:, c, h * S:(h + 1) * S] if t == 0 else PT[:, c, (4 + h) * P:(5 + h) * P]
                            last = pe.matmul(w[HD * j:HD * j + HD, t * P:S], pick[:, g, :], p, start=(g == 0 and t == 0),
                                             stop=(g == KT - 1 and t == TT - 1), skip_group_check=True)
                peA.done(last, "sum")

            def projected(b, t):
                if t == 0:
                    actA.wait(pe, "oh", b)
                    dveA.wait(pe, "ol", b)
                w = wkb(f"wo{t}", pe, b)
                tok = slice(t * P, (t + 1) * P)
                peA.done(products(w[:, :], [(a[:, g, tok], c[:, g, :]) for g in range(KT)
                                            for a, c in ((oh, WoTh), (oh, WoTl), (ol, WoTh))]), f"wo{t}")

            def mlp_in(b):
                dveB.wait(pe, "q", b)
                w = ffb("qxT", pe, b)[:, :].bitcast(BF16)
                for k in range(KT):
                    for t in range(TT):
                        last = pe.transpose(w[:, k * S + t * P:k * S + t * P + P], qx[:, t, k * P:(k + 1) * P], identb[:, :])
                peB.done(last, "qxT")
                dveB.wait(pe, "sp1", b)
                w = ffb("sxb", pe, b)
                for t in range(TT):
                    last = pe.matmul(w[:, t * P:(t + 1) * P], spread[:, t, :], ident[:, :], start=True, stop=True)
                peB.done(last, "sxb")

            def gate_up(b, n):
                if n == 0:
                    actB.wait(pe, "qxT", b)
                w = ffb(f"gu{n}", pe, b)
                i = slice(n * P, (n + 1) * P)
                products(w[:, 0:S], [(WgT[:, k, i], qxT[:, k, :]) for k in range(KT)])
                peB.done(products(w[:, S:], [(WuT[:, k, i], qxT[:, k, :]) for k in range(KT)]), f"gu{n}")

            def row_max(b):
                dveB.wait(pe, "ac1", b)
                w = ffb("amT", pe, b)
                for t in range(TT):
                    for n in range(2):
                        last = pe.transpose(w[:, (2 * t + n) * P:(2 * t + n + 1) * P], tmax[:, n, t * P:(t + 1) * P],
                                            ident[:, :])
                peB.done(last, "amT")

            def row_inv(b):
                dveB.wait(pe, "sq1", b)
                w = ffb("invb", pe, b)
                for t in range(TT):
                    last = pe.matmul(w[:, t * P:(t + 1) * P], spread2[:, t, :], ident[:, :], start=True, stop=True)
                peB.done(last, "invb")

            def down(b):
                w = [None, None]
                for h, half in enumerate(halves(IT)):
                    dveB.wait(pe, f"Q{h}", b)
                    for t in range(TT):
                        if h == 0:
                            w[t] = ffb(f"dn{t}", pe, b)
                        for i in range(half.start, half.stop):
                            last = pe.matmul(w[t][:, :], dq[:, 1, i, t * P:(t + 1) * P], WdT[:, i, :],
                                             start=(i == 0), stop=(i == IT - 1))
                        if h == 1:
                            peB.done(last, f"dn{t}")

            def iteration(l, p, a, b):
                if p is not None:
                    transposes(p)
                if a is not None:
                    scores(a, 0)
                    scores(a, 1)
                if p is not None:
                    keys(p, 0)
                    keys(p, 1)
                    queries(p, 0)
                if b is not None:
                    mlp_in(b)
                for n in range(IT):
                    if b is not None:
                        gate_up(b, n)
                    if p is not None and n == 1:
                        queries(p, 1)
                    if a is not None and n < NC - 2:
                        scores(a, n + 2)
                    if a is not None and n == NC - 1:
                        dveA.wait(pe, "m3", a)
                        w = wkb("mT", pe, a)[0:3 * TT * NH, 0:P // 2].bitcast(BF16)
                        peA.done(pe.transpose(w, m_parts[:, :, :].rearrange("p r n -> p (r n)"), identb[:, :]), "mT")
                if b is not None:
                    row_max(b)
                for c in range(NC):
                    if a is not None:
                        shifted(a, c)
                    if b is not None and c == 1:
                        row_inv(b)
                    if a is not None and c in (3, 5):
                        weighted(a, (c - 3) // 2)
                if a is not None:
                    weighted(a, KT - 2)
                    weighted(a, KT - 1)
                if p is not None:
                    values(p)
                if a is not None:
                    sums(a)
                if b is not None:
                    down(b)
                if a is not None:
                    projected(a, 0)
                    projected(a, 1)

            def mlp_weights():
                for n, (j, i, k) in enumerate(mlp_tiles()):
                    if i == 0:
                        dveF.wait(pe, f"q{j}", 0)
                    if n >= 2:
                        actF.wait(pe, f"t{n - 2}", 0)
                    w = ff[n % 2][:, :].bitcast(BF16)
                    for u in range(k):
                        for m in range(KT):
                            if j < 2:
                                dst = w[:, m * k * P + u * P:m * k * P + u * P + P]
                                src = wq8[:, (i + u) * H + m * P:(i + u) * H + m * P + P]
                            else:
                                dst = w[:, u * H + m * P:u * H + m * P + P]
                                src = wq8[:, m * I + (i + u) * P:m * I + (i + u) * P + P]
                            last = pe.transpose(dst, src, identb[:, :])
                    peF.done(last, f"t{n}")
                dveF.wait(pe, "spread", 0)
                actF.wait(pe, "t16", 0)
                for m in range(KT):
                    last = pe.matmul(ff[0][:, m * P:(m + 1) * P], cx[:, 0, m * P:(m + 1) * P], ident[:, :], start=True, stop=True)
                peF.done(last, "sc")
                dveF.wait(pe, "dsc", 0)

            pipeline(pe, iteration, mlp_weights)

        @block.scalar
        def _(act):
            def copy(dst, src):
                return act.activation(dst, src, ACT.Copy)

            peW.wait(act, "g", 0)
            actW.done(act.activation(tanh_g[:, :], att[0][:, 0:2], ACT.Tanh), "tanh")
            for n in range(10):
                peW.wait(act, f"a{n}", 0)
                actW.done(copy(w_parts[n][0], ring[n % 4][:, :]), f"a{n}")

            def take(b, progress, pe_progress, use, w, dst):
                pe_progress.wait(act, use, b)
                progress.done(copy(dst, w), use)

            def lift(progress, dve_progress, ready, value, dst, step, b):
                dve_progress.wait(act, ready, b)
                progress.done(act.activation(dst, value, ACT.Abs, scale=ROUND_LIFT), step)

            def flat2(t, j):
                return t[:, 2 * j:2 * j + 2, :].rearrange("p k s -> p (k s)")

            def high(b, use, w, dst):
                take(b, actP, peP, use, w, dst)

            def project(b):
                peP.wait(act, "q1", b - 1)
                for j in range(2):
                    high(b, f"xT{j}", wkb(f"xT{j}")[:, :], flat2(xTh, j))
                peP.wait(act, "v1", b - 1)
                high(b, "cT", wkb("cT")[:, 0:S], cTh[:, :])
                stack_k.wait(act, b - 1)
                for j in range(2):
                    high(b, f"k{j}", wkb(f"k{j}")[:, :], flat2(kh, j))

            def project_q(b, j):
                if j == 0:
                    stack_q.wait(act, b - 1)
                high(b, f"q{j}", wkb(f"q{j}")[:, :], flat2(qh, j))

            def project_v(b):
                peA.wait(act, "PV3", b - 1)
                for t in range(TT):
                    high(b, f"v{t}", wkb(f"v{t}")[:, :], V[:, t, :])

            def exps(b, c):
                if c == 0:
                    peA.wait(act, "sum", b - 1)
                peA.wait(act, f"ST{c}", b)
                actA.done(act.activation(PT[:, c, :], att[c % 2][:, 0:768], ACT.Exp, scale=SCALE), f"e{c}")

            def take_o(b, g):
                if g == 0:
                    dveA.wait(act, "on", b - 1)
                peA.wait(act, f"PV{g}", b)
                actA.done(copy(O[:, g, :], wkb(f"PV{g}")[:, 0:S]), f"O{g}")

            def lift_half(b, h):
                i = halves(IT)[h]
                lift(actB, dveB, f"X{h}", T[:, i, :], dq[:, 0, i, :], f"absT{h}", b)

            def iteration(l, p, a, b):
                if p is not None:
                    project(p)
                if b is not None:
                    lift(actB, dveB, "x1", cx[:, :, :], dx[:, :, :], "absx", b)
                if p is not None:
                    project_q(p, 0)
                if b is not None:
                    peB.wait(act, f"gu{IT - 1}", b - 1)
                    take(b, actB, peB, "qxT", ffb("qxT")[:, :].bitcast(BF16), qxT[:, :, :].rearrange("p k s -> p (k s)"))
                    dveB.wait(act, f"gs{IT - 1}", b - 1)
                    take(b, actB, peB, "sxb", ffb("sxb")[:, 0:S], sxb[:, :])
                for n in range(IT):
                    if b is not None:
                        dveB.wait(act, f"gs{n}", b)
                        if n >= 2:
                            dveB.wait(act, f"t{n - 2}", b)
                        actB.done(act.activation(sl[:, n % 2, :], gs[:, n % 2, :], ACT.Silu), f"silu{n}")
                    if p is not None and n == 1:
                        project_q(p, 1)
                    if a is not None and n == NC - 1:
                        stack_m.wait(act, a - 1)
                        take(a, actA, peA, "mT", wkb("mT")[0:3 * TT * NH, 0:P // 2].bitcast(BF16), mT[:, :])
                if a is not None:
                    exps(a, 0)
                    exps(a, 1)
                if b is not None:
                    dveB.wait(act, "X1", b - 1)
                    take(b, actB, peB, "invb", ffb("invb")[:, 0:S], tinvb[:, :])
                if a is not None:
                    exps(a, 2)
                    exps(a, 3)
                if b is not None:
                    lift_half(b, 0)
                if a is not None:
                    take_o(a, 0)
                    exps(a, 4)
                if b is not None:
                    lift_half(b, 1)
                if a is not None:
                    exps(a, 5)
                    take_o(a, 1)
                    exps(a, 6)
                    exps(a, 7)
                    take_o(a, 2)
                    take_o(a, 3)
                if p is not None:
                    project_v(p)
                if a is not None:
                    dveA.wait(act, "on", a)
                    peA.wait(act, "wo1", a - 1)
                    actA.done(copy(oh[:, :, :], R[:, :, :]), "oh")

            def mlp_weights():
                raws = (raw_gate, raw_up, raw_down)
                lift(actF, dveF, "x0", raws[0], wd, "abs0", 0)
                dveF.wait(act, "q0", 0)
                lift(actF, dveF, "x1", raws[1], wd, "abs1", 0)
                for n, (j, i, k) in enumerate(mlp_tiles()):
                    if n == 6:
                        dveF.wait(act, "q1", 0)
                        lift(actF, dveF, "x2", raws[2], wd, "abs2", 0)
                    peF.wait(act, f"t{n}", 0)
                    w = ff[n % 2][:, :].bitcast(BF16)
                    if j < 2:
                        dst = (WgT, WuT)[j][:, :, i * P:(i + k) * P]
                        src = w[:, 0:KT * k * P].rearrange("p (m f) -> p m f", m=KT)
                    else:
                        dst, src = WdT[:, i:i + k, :], w[:, 0:k * H].rearrange("p (u o) -> p u o", u=k)
                    actF.done(copy(dst, src), f"t{n}")

            pipeline(act, iteration, mlp_weights)

        @block.vector
        def _(dve):
            def low(dst, w, high):
                return dve.tensor_tensor(dst, w, high, ALU.subtract)

            for n in range(10):
                actW.wait(dve, f"a{n}", 0)
                dveW.done(low(w_parts[n][1], ring[n % 4][:, :], w_parts[n][0]), f"a{n}")

            def to_fp8(progress, b, value, lift, dst, steps, lifted):
                lifted(dve, b)
                progress.done(dve.tensor_scalar(lift, lift, ROUND_FLOOR * ROUND_LIFT, None, ALU.max), steps[1])
                progress.wait(dve, steps[1], b)
                progress.done(dve.tensor_tensor(value, value, lift, ALU.add), steps[2])
                progress.wait(dve, steps[2], b)
                progress.done(dve.tensor_tensor(dst, value, lift, ALU.subtract), steps[3])

            def mlp_matrix(j, raw, rows):
                n = (IT * H) // rows
                dve.wait_ge(s_raw[3 + j], 16 * (1 if j == 2 else IT))
                r = raw.rearrange("p (n f) -> p n f", n=n)
                dveF.done(dve.tensor_reduce(wmax[:, j, 0:n], r, AX.X, ALU.max, apply_absolute_value=True), f"mx{j}")
                dveF.wait(dve, f"mx{j}", 0)
                dveF.done(dve.reciprocal(winv[:, j, 0:n], wmax[:, j, 0:n]), f"rc{j}")
                dveF.wait(dve, f"rc{j}", 0)
                dveF.done(dve.tensor_scalar(winv[:, j, 0:n], winv[:, j, 0:n], FP8_MAX, None, ALU.mult), f"iv{j}")
                dveF.done(dve.tensor_scalar(wscale[:, j, 0:n], wmax[:, j, 0:n], 1.0 / FP8_MAX, None, ALU.mult), f"sc{j}")
                dveF.wait(dve, f"iv{j}", 0)
                for m in range(n):
                    last = dve.tensor_scalar(r[:, m, :], r[:, m, :], winv[:, j, m:m + 1], None, ALU.mult)
                dveF.done(last, f"x{j}")
                if j:
                    peF.wait(dve, f"t{6 * j - 1}", 0)
                to_fp8(dveF, 0, raw, wd, wq8, [f"x{j}", f"d{j}", f"y{j}", f"q{j}"],
                       lambda eng, b: actF.wait(eng, f"abs{j}", b))

            def norm1_stats(b):
                load_x.wait(dve, b)
                for t in range(TT):
                    dveL.done(dve.bn_stats(bn[:, t, :], xin[:, t, :]), f"st{t}")

            def norm1_mean(b):
                for t in range(TT):
                    dveL.wait(dve, f"st{t}", b)
                    apart(dve)
                    dveL.done(dve.bn_aggr(mv[:, t, :], bn[:, t, :]), f"ag{t}")

            def norm1(b):
                peP.wait(dve, "xT1", b - 1)
                poolL.wait(dve, "rs", b)
                for t in range(TT):
                    dveL.done(dve.tensor_scalar(xn[:, t, :], xin[:, t, :], mv[:, t, 0:1], rstd[:, t:t + 1],
                                                ALU.subtract, ALU.mult), f"xn{t}")

            def take_low(b, use, w, dst, high):
                actP.wait(dve, use, b)
                dveP.done(low(dst, w, high), use)

            def take2(b, use, dst, high):
                j = int(use[-1])
                take_low(b, use, wkb(use)[:, :], dst[:, 2 * j:2 * j + 2, :].rearrange("p k s -> p (k s)"),
                         high[:, 2 * j:2 * j + 2, :].rearrange("p k s -> p (k s)"))

            def maxima(b, c):
                peA.wait(dve, f"S{c}", b)
                w = att[c % 2]
                dveA.done(dve.tensor_reduce(mx[:, 2 * c:2 * c + 2, 0], w[:, 0:2 * P].rearrange("p (h k) -> p h k", h=2),
                                            AX.X, ALU.max), f"mx{c}a")
                dveA.done(dve.tensor_reduce(mx[:, 2 * c:2 * c + 2, 1],
                                            w[:, 2 * P:6 * P].rearrange("p (r h k) -> p h r k", r=2, h=2),
                                            AX.XY, ALU.max), f"mx{c}b")

            def max_parts(b):
                dveA.wait(dve, f"mx{NC - 1}b", b)
                m = mx[:, :, :].rearrange("p h t -> p (h t)")
                dveA.done(dve.tensor_scalar(m_parts[:, 0, :], m, -1.0, None, ALU.mult), "m1")
                dveA.wait(dve, "m1", b)
                dveA.done(dve.scalar_tensor_tensor(out=m_rest[:, 0, :], in0=m, scalar=-1.0, in1=m_parts[:, 0, :],
                                                   op0=ALU.mult, op1=ALU.subtract), "r1")
                dveA.wait(dve, "r1", b)
                dveA.done(dve.tensor_copy(m_parts[:, 1, :], m_rest[:, 0, :]), "m2")
                dveA.wait(dve, "m2", b)
                dveA.done(dve.tensor_tensor(m_parts[:, 2, :], m_rest[:, 0, :], m_parts[:, 1, :], ALU.subtract), "m3")

            def normalise(b):
                peA.wait(dve, "sum", b)
                dveA.done(dve.reciprocal(rsum[:, :], wkb("sum")[:, 0:S]), "rc")
                dveA.wait(dve, "rc", b)
                apart(dve)
                for g in range(KT):
                    dveA.done(dve.stream_shuffle(out=R[:, g, :], in_=rsum[:, :], mask=[g] * HD), f"sh{g}")
                actA.wait(dve, "O3", b)
                dveA.wait(dve, "sh3", b)
                dveA.done(dve.tensor_tensor(R[:, :, :], O[:, :, :], R[:, :, :], ALU.mult), "on")
                actA.wait(dve, "oh", b)
                dveA.done(low(ol[:, :, :], R[:, :, :], oh[:, :, :]), "ol")

            def residual(b):
                load_res.wait(dve, b)
                poolB.wait(dve, "o1", b - 1)
                for t in range(TT):
                    peA.wait(dve, f"wo{t}", b)
                    dveA.done(dve.scalar_tensor_tensor(out=x1[:, t, :], in0=wkb(f"wo{t}")[:, :], scalar=tanh_g[:, 0:1],
                                                       in1=xres[:, t, :], op0=ALU.mult, op1=ALU.add), f"x1_{t}")

            def norm2_stats(b):
                for t in range(TT):
                    dveA.wait(dve, f"x1_{t}", b)
                    dveB.done(dve.bn_stats(bn2[:, t, :], x1[:, t, :]), f"st{t}")
                for t in range(TT):
                    dveB.wait(dve, f"st{t}", b)
                    apart(dve)
                    dveB.done(dve.bn_aggr(mv2[:, t, :], bn2[:, t, :]), f"ag{t}")
                for t in range(TT):
                    dveB.wait(dve, f"ag{t}", b)
                    dveB.done(dve.tensor_scalar(cx[:, t, :], x1[:, t, :], mv2[:, t, 0:1], None, ALU.subtract), f"c{t}")

            def norm2_scales(b):
                dveB.wait(dve, "c1", b)
                dveB.done(dve.tensor_reduce(amax[:, :], cx[:, :, :], AX.X, ALU.max, apply_absolute_value=True), "am")
                poolB.wait(dve, "rs", b)
                dveB.wait(dve, "am", b)
                dveB.done(dve.tensor_tensor(sx[:, :], amax[:, :], rstd2[:, :], ALU.mult), "sx0")
                dveB.wait(dve, "sx0", b)
                dveB.done(dve.tensor_scalar(sx[:, :], sx[:, :], 1.0 / FP8_MAX, None, ALU.mult), "sx1")
                dveB.done(dve.reciprocal(ainv[:, :], amax[:, :]), "rc")
                dveB.wait(dve, "rc", b)
                dveB.done(dve.tensor_scalar(ainv[:, :], ainv[:, :], FP8_MAX, None, ALU.mult), "iv")
                dveB.wait(dve, "iv", b)
                for t in range(TT):
                    dveB.done(dve.tensor_scalar(cx[:, t, :], cx[:, t, :], ainv[:, t:t + 1], None, ALU.mult), f"x{t}")

            def norm2_fp8(b):
                peB.wait(dve, "qxT", b - 1)
                to_fp8(dveB, b, cx[:, :, :], dx[:, :, :], qx[:, :, :], ["x1", "d", "y", "q"],
                       lambda eng, b: actB.wait(eng, "absx", b))
                peB.wait(dve, "sxb", b - 1)
                for t in range(TT):
                    dveB.done(dve.tensor_scalar(spread[:, t, :], ones[:, :], sx[:, t:t + 1], None, ALU.mult), f"sp{t}")

            def gate(b, n):
                if n == 0:
                    actB.wait(dve, "sxb", b)
                peB.wait(dve, f"gu{n}", b)
                if n >= 2:
                    actB.wait(dve, f"silu{n - 2}", b)
                dveB.done(dve.scalar_tensor_tensor(out=gs[:, n % 2, :], in0=ffb(f"gu{n}")[:, 0:S], scalar=wscale[:, 0, n:n + 1],
                                                   in1=sxb[:, :], op0=ALU.mult, op1=ALU.mult), f"gs{n}")

            def up(b, n):
                if n == 0:
                    peB.wait(dve, "dn1", b - 1)
                actB.wait(dve, f"silu{n}", b)
                dveB.done(dve.scalar_tensor_tensor(out=T[:, n, :], in0=ffb(f"gu{n}")[:, S:], scalar=wscale[:, 1, n:n + 1],
                                                   in1=sl[:, n % 2, :], op0=ALU.mult, op1=ALU.mult), f"t{n}")

            def largest(b, n):
                first, last = [(h.start, h.stop) for h in halves(IT)][n]
                dveB.wait(dve, f"t{last - 1}", b)
                if n == 0:
                    peB.wait(dve, "amT", b - 1)
                dveB.done(dve.tensor_reduce(tmax[:, n, :], T[:, first:last, :].rearrange("p i s -> p s i"), AX.X, ALU.max,
                                            apply_absolute_value=True), f"ac{n}")

            def mlp_scales(b):
                peB.wait(dve, "amT", b)
                dveB.done(dve.tensor_reduce(tm[:, :], ffb("amT")[:, :].rearrange("p (t i) -> p t i", t=TT), AX.X, ALU.max), "mt")
                dveB.wait(dve, "mt", b)
                dveB.done(dve.tensor_tensor(st[:, :], tm[:, :], sx[:, :], ALU.mult), "st_a")
                dveB.wait(dve, "st_a", b)
                dveB.done(dve.tensor_scalar(st[:, :], st[:, :], 1.0 / FP8_MAX, None, ALU.mult), "st_b")
                dveB.done(dve.reciprocal(tinv[:, :], tm[:, :]), "rc2")
                dveB.wait(dve, "rc2", b)
                dveB.done(dve.tensor_scalar(tinv[:, :], tinv[:, :], FP8_MAX, None, ALU.mult), "iv2")
                dveB.wait(dve, "iv2", b)
                peB.wait(dve, "invb", b - 1)
                for t in range(TT):
                    dveB.done(dve.tensor_scalar(spread2[:, t, :], ones[:, :], tinv[:, t:t + 1], None, ALU.mult), f"sq{t}")

            def mlp_fp8(b):
                actB.wait(dve, "invb", b)
                dveB.wait(dve, "ac1", b)
                for h, i in enumerate(halves(IT)):
                    n = i.stop - i.start
                    dveB.done(dve.tensor_tensor(T[:, i, :], T[:, i, :], tinvb[:, :].unsqueeze(1).to_broadcast([P, n, S]),
                                                ALU.mult), f"X{h}")
                for h, i in enumerate(halves(IT)):
                    to_fp8(dveB, b, T[:, i, :], dq[:, 0, i, :], dq[:, 1, i, :], [f"X{h}", f"D{h}", f"Y{h}", f"Q{h}"],
                           lambda eng, b: actB.wait(eng, f"absT{h}", b))

            def mlp_out(b, t):
                peB.wait(dve, f"dn{t}", b)
                poolB.wait(dve, f"o{t}", b - 1)
                dveB.done(dve.scalar_tensor_tensor(out=yb[:, t, :], in0=ffb(f"dn{t}")[:, :], scalar=st[:, t:t + 1],
                                                   in1=down_scale[:, :], op0=ALU.mult, op1=ALU.mult), f"y{t}")

            def iteration(l, p, a, b):
                if b is not None:
                    norm2_stats(b)
                if p is not None:
                    peP.wait(dve, "q1", p - 1)
                    take2(p, "xT0", xTl, xTh)
                    take2(p, "xT1", xTl, xTh)
                    peP.wait(dve, "v1", p - 1)
                    take_low(p, "cT", wkb("cT")[:, 0:S], cTl[:, :], cTh[:, :])
                if b is not None:
                    norm2_scales(b)
                if a is not None:
                    maxima(a, 0)
                    maxima(a, 1)
                if p is not None:
                    stack_k.wait(dve, p - 1)
                    take2(p, "k0", kl, kh)
                    take2(p, "k1", kl, kh)
                if b is not None:
                    norm2_fp8(b)
                for n in range(IT + 2):
                    if b is not None:
                        for step, m in mlp_order(IT, n):
                            {"gs": gate, "t": up, "ac": largest}[step](b, m)
                    if p is not None and n in (0, 3):
                        if n == 0:
                            stack_q.wait(dve, p - 1)
                        take2(p, f"q{n // 3}", ql, qh)
                    if a is not None and n < NC - 2:
                        maxima(a, n + 2)
                    if a is not None and n == NC - 2:
                        max_parts(a)
                if l is not None:
                    norm1_stats(l)
                if b is not None:
                    mlp_scales(b)
                if l is not None:
                    norm1_mean(l)
                if b is not None:
                    mlp_fp8(b)
                if a is not None:
                    normalise(a)
                if b is not None:
                    mlp_out(b, 0)
                    mlp_out(b, 1)
                if l is not None:
                    norm1(l)
                if a is not None:
                    residual(a)

            def mlp_weights():
                mlp_matrix(0, raw_gate, H)
                mlp_matrix(1, raw_up, H)
                mlp_matrix(2, raw_down, I)
                dveF.wait(dve, "q2", 0)
                for m in range(KT):
                    last = dve.tensor_scalar(cx[:, 0, m * P:(m + 1) * P], ones[:, :], wscale[:, 2, m:m + 1], None, ALU.mult)
                dveF.done(last, "spread")
                peF.wait(dve, "sc", 0)
                actW.wait(dve, "tanh", 0)
                dveF.done(dve.tensor_scalar(down_scale[:, :], ff[0][:, :], tanh_g[:, 1:2], None, ALU.mult), "dsc")
                dveF.wait(dve, "dsc", 0)

            dve.wait_ge(s_const, N_CONST)
            norm1_stats(0)
            norm1_mean(0)
            norm1(0)
            pipeline(dve, iteration, mlp_weights)


def halves(n_tiles):
    return slice(0, (n_tiles + 1) // 2), slice((n_tiles + 1) // 2, n_tiles)


def mlp_order(n_tiles, n):
    halves = {7: 0, n_tiles + 1: 1}
    return ([(s, m) for s, m in (("gs", n), ("t", n - 1)) if 0 <= m < n_tiles]
            + ([("ac", halves[n])] if n in halves else []))


def mlp_steps(n_tiles):
    return [f"{s}{m}" for n in range(n_tiles + 2) for s, m in mlp_order(n_tiles, n)]


_INS = ["x", "ctx_512", "g_xattn", "g_ffn", "L0_xattn_Wq", "L0_xattn_Wkv_expand", "L0_xattn_Wout",
        "L0_ffn_w_gate", "L0_ffn_w_up", "L0_ffn_w_down", "L0_ffn_down_reorder_index"]


def kernel(**inputs):
    import numpy as _np
    import concourse.bacc as _bacc
    from concourse import mybir as _mybir
    from concourse.bass_utils import run_bass_kernel_spmd as _run

    nc = _bacc.Bacc("TRN2", target_bir_lowering=False, num_devices=1)
    arrays, args = {}, []
    for name in _INS:
        a = _np.ascontiguousarray(inputs[name])
        arrays[f"in_{name}_dram"] = a
        args.append(nc.dram_tensor(f"in_{name}_dram", a.shape, _mybir.dt.from_np(a.dtype), kind="ExternalInput").ap())
    args.append(nc.dram_tensor("out_0_dram", inputs["x"].shape, F32, kind="ExternalOutput").ap())
    gated_block_kernel(nc, *args)
    r = _run(nc, [arrays], core_ids=[0])
    return r.results[0]["out_0_dram"]
```

```python
from contextlib import ExitStack

import concourse.bass as bass
from concourse import mybir

P = 128
FP8_MAX = 448.0
ROUND_FLOOR = 1.5 * 2.0**-6
ROUND_LIFT = 2.0**20
LN_EPS = 1e-5
MASKED = -3.3e38

F32 = mybir.dt.float32
BF16 = mybir.dt.bfloat16
ALU = mybir.AluOpType
ACT = mybir.ActivationFunctionType
AX = mybir.AxisListType


class Progress:

    def __init__(self, sem, steps):
        self.sem = sem
        self.steps = list(steps)
        self.at = 0

    def done(self, instruction, step):
        assert self.steps[self.at % len(self.steps)] == step, (step, self.steps[self.at % len(self.steps)])
        self.at += 1
        instruction.then_inc(self.sem, 1)

    def wait(self, eng, step, b):
        value = b * len(self.steps) + self.steps.index(step) + 1
        if isinstance(value, int) and value <= 0:
            return
        eng.wait_ge(self.sem, value)


class Loads:

    def __init__(self, sem, n):
        self.sem = sem
        self.n = n

    def started(self, dma):
        dma.then_inc(self.sem, 16)

    def wait(self, eng, b):
        value = (b + 1) * (16 * self.n)
        if isinstance(value, int) and value <= 0:
            return
        eng.wait_ge(self.sem, value)


def names(prefix, n):
    return [f"{prefix}{i}" for i in range(n)]


def gated_block_kernel(nc, x, ctx_in, g_x, g_f, w_q, w_kv, w_out, w_gate, w_up, w_down, down_index, out):
    NB, S, H = x.shape
    L = ctx_in.shape[2]
    I = w_gate.shape[0]
    HD = 32
    NH = H // HD
    TT = S // P
    KT = H // P
    IT = I // P
    G = P // HD
    NC = NH // 2
    SCALE = float(HD) ** -0.5
    PAIRS = pairs(IT)
    UNITS = [(j, i, min(2, IT - i)) for j in range(2) for i in range(0, IT, 2)] + [(2, m, 1) for m in range(KT)]
    N_ROUNDS = len(UNITS) + 2
    ROUNDS = {("start", 0): (0, 1), (1, "x"): (2,), (1, "k"): (3,), (1, "q"): (4,), (1, "m"): (5,), (1, "v"): (6,),
              (1, "end"): (7, 8), (2, "x"): (9,), (2, "k"): (10,), (2, "q"): (11,), (2, "m"): (12, 13), (2, "e"): (14,),
              (2, "s"): (15,), (2, "v"): (16,), (2, "end"): (17,)}
    assert sum(len(v) for v in ROUNDS.values()) == N_ROUNDS
    TURNS = [(u, i, k) for u, (j, i, k) in enumerate(UNITS) if j < 2]
    TURNS += [(u, i, n) for u, (j, m, k) in enumerate(UNITS) if j == 2 for i, n in ((0, 6), (6, IT - 6))]
    assert (TT, L, KT * P, IT * P) == (2, P, H, I) and KT == 4 and G == 4

    with ExitStack() as stack:
        def sb(name, shape, dt=F32):
            return stack.enter_context(nc.sbuf_tensor(name, shape, dt))

        def sem(name):
            return stack.enter_context(nc.semaphore(name))

        att = [stack.enter_context(nc.psum_tensor(f"att{i}", [P, 1024], F32)) for i in range(2)]
        wk = [stack.enter_context(nc.psum_tensor(f"wk{i}", [P, 512], F32)) for i in range(2)]
        ff = [stack.enter_context(nc.psum_tensor(f"ff{i}", [P, 512], F32)) for i in range(2)]

        ident = sb("ident", [P, P])
        identb = sb("identb", [P, P], BF16)
        minus_identb = sb("minus_identb", [P, P], BF16)
        ones = sb("ones", [P, P])
        causal4 = sb("causal4", [P, 4, P], BF16)
        pick = sb("pick", [P, KT, HD])
        minus_half = sb("minus_half", [P, TT])
        gates = sb("gates", [1, 2])
        tanh_g = sb("tanh_g", [P, 2])
        index = sb("index", [P, IT], mybir.dt.int32)

        WqTh = sb("WqTh", [P, KT, H], BF16)
        WqTl = sb("WqTl", [P, KT, H], BF16)
        WkvTh = sb("WkvTh", [P, 2 * H], BF16)
        WkvTl = sb("WkvTl", [P, 2 * H], BF16)
        WoTh = sb("WoTh", [P, KT, H], BF16)
        WoTl = sb("WoTl", [P, KT, H], BF16)
        WgT = sb("WgT", [P, KT, I], BF16)
        WuT = sb("WuT", [P, KT, I], BF16)
        WdT = sb("WdT", [P, IT, H], BF16)
        wscale = sb("wscale", [P, 3, IT])
        wmax = sb("wmax", [P, 3, IT])
        winv = sb("winv", [P, 3, IT])
        wlift = sb("wlift", [P, 3, IT])
        down_scale = sb("down_scale", [P, H])

        xin = sb("xin", [P, TT, H])
        cin = sb("cin", [P, TT, L])
        xres = sb("xres", [P, TT, H])
        bn = sb("bn", [P, TT, 6])
        mv = sb("mv", [P, TT, 2])
        var_eps = sb("var_eps", [P, TT])
        rstd = sb("rstd", [P, TT])
        mean_minus = sb("mean_minus", [P, TT])
        shift = sb("shift", [P, TT])
        xn = sb("xn", [P, TT, H])
        xTh = sb("xTh", [P, KT, S], BF16)
        xTl = sb("xTl", [P, KT, S], BF16)
        cTh = sb("cTh", [P, S], BF16)
        cTl = sb("cTl", [P, S], BF16)
        kh = sb("kh", [P, KT, S], BF16)
        kl = sb("kl", [P, KT, S], BF16)
        qh = sb("qh", [P, KT, S], BF16)
        ql = sb("ql", [P, KT, S], BF16)
        V = sb("V", [P, TT, H])
        Q4 = sb("Q4", [P, NH, S], BF16)
        K4 = sb("K4", [P, NH, S], BF16)
        mx = sb("mx", [P, NH, TT])
        m_parts = sb("m_parts", [P, 3, TT * NH], BF16)
        m_rest = sb("m_rest", [P, 2, TT * NH])
        mT = sb("mT", [3 * TT * NH, P], BF16)
        PT = sb("PT", [P, NC, 768])
        O = sb("O", [P, KT, S])
        rsum = sb("rsum", [P, S])
        R = sb("R", [P, KT, S])
        oh = sb("oh", [P, KT, S], BF16)
        ol = sb("ol", [P, KT, S], BF16)
        x1 = sb("x1", [P, TT, H])
        bn2 = sb("bn2", [P, TT, 6])
        mv2 = sb("mv2", [P, TT, 2])
        var_eps2 = sb("var_eps2", [P, TT])
        rstd2 = sb("rstd2", [P, TT])
        mean_minus2 = sb("mean_minus2", [P, TT])
        amax = sb("amax", [P, TT])
        ainv = sb("ainv", [P, TT])
        sx = sb("sx", [P, TT])
        T = sb("T", [P, IT, S])
        dq = sb("dq", [P, 2, IT, S], BF16)
        tmax = sb("tmax", [P, 2, S])
        tm = sb("tm", [P, TT])
        tinv = sb("tinv", [P, TT])
        st = sb("st", [P, TT])
        ob = sb("ob", [P, TT, H])

        sl = sb("sl", [P, 4, S])

        raw_a = sb("raw_a", [P, IT * H])
        carved = [0]

        def carve(a, n, dt=F32):
            words = a * n * (2 if dt == BF16 else 4) // 4
            at, carved[0] = carved[0], carved[0] + words
            part = raw_a[:, at:at + words]
            part = part.bitcast(dt) if dt == BF16 else part
            return part.rearrange("p (a n) -> p a n", a=a)

        cx = carve(TT, H)
        dx = carve(TT, H, BF16)
        qx = carve(TT, H, BF16)
        qxT = carve(KT, S, BF16)
        gs = carve(4, S)
        yb = carve(TT, H)
        spread = carve(TT, P)
        spread2 = carve(TT, P)
        sxb = raw_a[:, carved[0]:carved[0] + S]
        assert carved[0] + S <= IT * H
        raw_q = PT[:, :, :].rearrange("p c n -> p (c n)")[:, 0:KT * H].rearrange("p (m h) -> p m h", m=KT)
        raw_kv = xn[:, :, :].rearrange("p t h -> p (t h)").rearrange("p (m l) -> p m l", l=L)
        raw_o = raw_a[:, 0:KT * H].rearrange("p (m h) -> p m h", m=KT)
        wd = T[:, :, :].bitcast(BF16).rearrange("p i s -> p (i s)")
        wq8 = dq[:, :, :, :].rearrange("p a i s -> p (a i s)")

        s_const = sem("s_const")
        s_index = sem("s_index")
        s_apart = sem("s_apart")
        s_gates = sem("s_gates")
        s_raw = [sem(f"s_raw_{n}") for n in ("q", "kv", "o")]
        s_unit = [sem(f"s_unit{u}") for u in range(len(UNITS))]
        peW = Progress(sem("peW"), ["g"] + names("a", 10))
        actW = Progress(sem("actW"), ["tanh"] + names("a", 10))
        dveW = Progress(sem("dveW"), names("a", 10))
        dveF = Progress(sem("dveF"), weight_steps(len(UNITS), ("mx", "rc", "iv", "lf", "sc"), ("d", "y", "q")) + ["spread", "dsc"])
        poolF = Progress(sem("poolF"), weight_steps(len(UNITS), (), ("y", "q")))
        peF = Progress(sem("peF"), names("t", len(TURNS)) + ["sc"])
        actF = Progress(sem("actF"), [s for r in range(N_ROUNDS) for s in ([f"lift{r}", f"x{r}"] if r < len(UNITS) else [])
                                      + [f"t{n}" for n, turn in enumerate(TURNS) if turn[0] == r - 2]])

        load_x = Loads(sem("load_x"), 2)
        load_res = Loads(sem("load_res"), 1)
        stack_k = Loads(sem("stack_k"), 3)
        stack_q = Loads(sem("stack_q"), 4)
        stack_m = Loads(sem("stack_m"), 1)
        store = Loads(sem("store"), 1)

        proj = ["xT0", "xT1", "cT", "k0", "k1", "q0", "q1"]
        order = ["xT0", "xT1", "xT0{}", "xT1{}", "cT", "cT{}", "k0", "k1", "k0{}", "k1{}", "q0", "q0{}", "q1", "q1{}"]
        peP = Progress(sem("peP"), [u.format("m") for u in order] + ["v0", "v1"])
        peS = Progress(sem("peS"), ["S0", "S1"])
        peA = Progress(sem("peA"), names("S", NC)[2:] + ["mT", "ST0", "ST1", "ST2", "ST3", "ST4", "ST5", "PV0", "ST6",
                                                     "ST7", "PV1", "PV2", "PV3", "sum", "wo0", "wo1"])
        peB = Progress(sem("peB"), ["qxT", "sxb"] + gate_up_steps(len(PAIRS)) + ["amT", "invb", "dn0", "dn1"])
        dveL = Progress(sem("dveL"), ["st0", "st1", "ag0", "ag1"])
        dveS = Progress(sem("dveS"), [f"mx{c}{h}" for c in range(2) for h in "ab"])
        dveA = Progress(sem("dveA"), [f"mx{c}{h}" for c in range(2, NC) for h in "ab"]
                        + ["m1", "r1", "m2", "m3", "rc"] + names("sh", KT) + ["on0", "on1", "ol0", "ol1", "x1_0", "x1_1"])
        dveB = Progress(sem("dveB"), ["st0", "ag0", "nm0", "st1", "ag1", "nm1", "am0", "am1", "rc", "x0", "x1", "sx0", "sx1",
                                      "d", "y", "q", "sp0", "sp1"]
                        + mlp_steps(IT) + ["mt", "rc2", "sq0", "sq1", "st_a", "st_b",
                                           "X0", "X1", "D0", "Y", "D1", "Q"])
        actL = Progress(sem("actL"), ["xn0", "xn1"])
        actP = Progress(sem("actP"), [u.format("l") for u in order] + ["v0", "v1"])
        actA = Progress(sem("actA"), ["mT", "e0", "e1", "e2", "e3", "e4", "e5", "O0", "e6", "e7", "O1", "O2", "O3", "oh0", "oh1"])
        actB = Progress(sem("actB"), ["c0", "c1", "absx", "qxT", "sxb"] + names("silu", len(PAIRS)) + ["absT0", "absT1"])
        dveO = Progress(sem("dveO"), ["y0", "y1"])
        poolO = Progress(sem("poolO"), ["o0", "o1"])
        poolL = Progress(sem("poolL"), ["ve", "rs", "nm", "nb"])
        poolA = Progress(sem("poolA"), [f"sel{c}{h}" for c in range(NC) for h in "ab"])
        poolB = Progress(sem("poolB"), ["ve", "rs", "y", "q", "cp", "Y", "Q"])

        wk_uses = proj + ["mT", "PV0", "PV1", "PV2", "PV3", "sum", "v0", "v1", "wo0", "wo1"]
        wk_freed = {n: (actP, f"{n}l") for n in proj}
        wk_freed |= {"v0": (actP, "v0"), "v1": (actP, "v1"), "mT": (actA, "mT"), "sum": (dveA, "rc")}
        wk_freed |= {f"PV{g}": (actA, f"O{g}") for g in range(KT)} | {f"wo{t}": (dveA, f"x1_{t}") for t in range(TT)}
        ff_uses = ["qxT", "sxb"] + [s + str(j) for j in range(len(PAIRS)) for s in ("ga", "up")] + ["amT", "invb", "dn0", "dn1"]
        ff_freed = {"qxT": (actB, "qxT"), "sxb": (actB, "sxb"), "amT": (dveB, "mt"), "invb": (dveB, "X1"),
                    "dn0": (dveO, "y0"), "dn1": (dveO, "y1")} | {f"ga{j}": (dveB, f"gs{pair[-1]}") for j, pair in enumerate(PAIRS)}
        ff_freed |= {f"up{j}": (dveB, f"t{pair[-1]}") for j, pair in enumerate(PAIRS)}

        def bank(banks, uses, freed, use, eng=None, b=None):
            ahead = lambda u: 1 if u in proj or u in ("v0", "v1") else 0
            n = uses.index(use)
            if eng is not None:
                at = b - (ahead(use) if uses is wk_uses else 0)
                same = [m for m in range(len(uses) - 1, -1, -1) if m % 2 == n % 2]
                for m, lag in [(m, 0) for m in same if m < n] + [(m, lag) for lag in (1, 2) for m in same]:
                    batch = at - lag + (ahead(uses[m]) if uses is wk_uses else 0)
                    if not isinstance(batch, int) or 0 <= batch < NB:
                        progress, step = freed[uses[m]]
                        progress.wait(eng, step, batch)
                        break
            return banks[n % 2]

        def wkb(use, eng=None, b=None):
            return bank(wk, wk_uses, wk_freed, use, eng, b)

        def ffb(use, eng=None, b=None):
            return bank(ff, ff_uses, ff_freed, use, eng, b)

        N_CONST_FIRST = 3
        N_CONST = 13 + KT + 1

        def apart(eng):
            eng.sem_inc(s_apart, 1)

        def unit_span(u):
            j, i, k = UNITS[u]
            width = H if j < 2 else I
            return slice(i * width, (i + k) * width), [slice((i + n) * width, (i + n + 1) * width) for n in range(k)]

        def unit_shares(u):
            span, tiles = unit_span(u)
            middle = (span.start + span.stop) // 2
            return slice(span.start, middle), slice(middle, span.stop)

        def overlapped(u):
            span, j = unit_span(u)[0], UNITS[u][0]
            before = [v for v in range(u) if UNITS[v][0] == j - 1 and unit_span(v)[0].start < span.stop]
            return before[-1] if before else None

        def place(head):
            return head % G * KT + head // G

        def last_turn(u):
            return max(n for n, turn in enumerate(TURNS) if turn[0] == u)

        def between(weight_round, l, place):
            if isinstance(l, int):
                for n in ROUNDS.get((l, place), ()):
                    weight_round(n)

        def flat2(t, j):
            return t[:, 2 * j:2 * j + 2, :].rearrange("p k s -> p (k s)")

        block = stack.enter_context(nc.Block())

        def pipeline(eng, iteration, weight_round, last_weights):
            for n in ROUNDS["start", 0]:
                weight_round(n)
            iteration(1, 0, None, None, None)
            iteration(2, 1, 0, None, None)
            last_weights()
            iteration(3, 2, 1, 0, None)
            iteration(4, 3, 2, 1, 0)
            with eng.Fori(3, NB - 2) as i:
                iteration(i + 2, i + 1, i, i - 1, i - 2)
            iteration(None, NB - 1, NB - 2, NB - 3, NB - 4)
            iteration(None, None, NB - 1, NB - 2, NB - 3)
            iteration(None, None, None, NB - 1, NB - 2)
            iteration(None, None, None, None, NB - 1)

        @block.sync
        def _(sp):
            def load_tokens(b):
                actL.wait(sp, "xn1", b - 1)
                apart(sp)
                load_x.started(sp.dma_start(xin[:, :, :], x[b].rearrange("(t p) h -> p t h", p=P)))

            def load_context(b):
                peP.wait(sp, "cT", b - 1)
                apart(sp)
                load_x.started(sp.dma_start(cin[:, :, :], ctx_in[b].rearrange("(t p) l -> p t l", p=P)))

            sp.dma_start(gates[0:1, 0:1], g_x.rearrange("(a n) -> a n", a=1)).then_inc(s_gates, 16)
            sp.dma_start(gates[0:1, 1:2], g_f.rearrange("(a n) -> a n", a=1)).then_inc(s_gates, 16)
            sp.dma_start(raw_kv, w_kv.rearrange("(m p) l -> p m l", p=P)).then_inc(s_raw[1], 16)
            sp.dma_start(raw_q, w_q.rearrange("(m p) h -> p m h", p=P)).then_inc(s_raw[0], 16)
            sp.dma_start(raw_o, w_out.rearrange("(m p) h -> p m h", p=P)).then_inc(s_raw[2], 16)
            load_tokens(0)
            load_context(0)

            def iteration(l, p, a, b, o):
                if l is not None:
                    load_tokens(l)
                if a is not None:
                    dveA.wait(sp, "x1_1", a - 1)
                    apart(sp)
                    load_res.started(sp.dma_start(xres[:, :, :], x[a].rearrange("(t p) h -> p t h", p=P)))
                if l is not None:
                    load_context(l)
                if o is not None:
                    poolO.wait(sp, "o1", o)
                    apart(sp)
                    store.started(sp.dma_start(out[o].rearrange("(t p) h -> p t h", p=P), ob[:, :, :]))
                if a is not None:
                    actA.wait(sp, "mT", a)
                    apart(sp)
                    stack_m.started(sp.dma_start(Q4[96:99, :, :].rearrange("r h (t s) -> r (h t) s", t=TT), mT[:, :]))
                if p is not None:
                    Q5 = Q4[:, :, :].rearrange("p (j g) s -> p j (g s)", j=G)
                    K5 = K4[:, :, :].rearrange("p (j g) s -> p j (g s)", j=G)
                    actP.wait(sp, "k1l", p)
                    apart(sp)
                    peA.wait(sp, "ST7", p - 1)
                    apart(sp)
                    for part, (keys, queries) in enumerate(((kh, qh), (kh, ql), (kl, qh))):
                        rows = slice(HD * part, HD * part + HD)
                        if part == 0:
                            stack_q.started(sp.dma_start(Q4[96:99, :, :], K4[99:102, :, :]))
                        stack_k.started(sp.dma_start(K5[rows], keys[:, :, :].rearrange("p g s -> p (g s)")))
                        if part == 0:
                            actP.wait(sp, "q1l", p)
                            apart(sp)
                        stack_q.started(sp.dma_start(Q5[rows], queries[:, :, :].rearrange("p g s -> p (g s)")))

            pipeline(sp, iteration, lambda n: None, lambda: None)
            store.wait(sp, NB - 1)


        @block.gpsimd
        def _(pool):
            n_const = [0]

            def const(instruction):
                instruction.then_inc(s_const, 1)
                n_const[0] += 1
                pool.wait_ge(s_const, n_const[0])

            def unit(m, one):
                const(pool.memset(m[:, :], 0.0))
                const(pool.affine_select(out=m[:, :], in_=m[:, :], compare_op=ALU.not_equal, fill=one,
                                         base=0, pattern=[[-1, P]], channel_multiplier=1))

            unit(ident, 1.0)
            const(pool.memset(ones[:, :], 1.0))
            assert n_const[0] == N_CONST_FIRST
            unit(identb, 1.0)
            unit(minus_identb, -1.0)
            const(pool.memset(minus_half[:, :], -0.5))
            pool.dma_start(index[:, :], down_index.rearrange("(i p) -> p i", p=P), allow_slow_non_contiguous=True)\
                .then_inc(s_index, 16)
            const(pool.memset(causal4[:, :, :], 0.0))
            const(pool.affine_select(out=causal4[:, :, :], in_=causal4[:, :, :], compare_op=ALU.is_ge, fill=MASKED,
                                     base=0, pattern=[[0, 4], [-1, P]], channel_multiplier=1))
            const(pool.memset(pick[:, :, :], 0.0))
            for g in range(KT):
                const(pool.memset(pick[:, g, :].rearrange("p (a b) -> p a b", b=4)[:, :, g:g + 1], 1.0))
            const(pool.memset(Q4[96:128, :, :], 0.0))
            const(pool.memset(K4[96:128, :, :], 0.0))
            const(pool.memset(K4[96:99, :, :], 1.0))
            assert n_const[0] == N_CONST

            def gather(u):
                j, i, k = UNITS[u]
                before = overlapped(u)
                if before is not None:
                    dveF.wait(pool, f"q{before}", 0)
                    poolF.wait(pool, f"q{before}", 0)
                span, tiles = unit_span(u)
                if j == 2:
                    pool.dma_start(raw_a[:, span], w_down[i * P:(i + 1) * P, :]).then_inc(s_unit[u], 16)
                for n, tile in enumerate(tiles if j < 2 else ()):
                    pool.indirect_dma_start(
                        out=raw_a[:, tile], out_offset=None, in_=(w_gate, w_up)[j][:, :],
                        in_offset=bass.IndirectOffsetOnAxis(ap=index[:, i + n:i + n + 1], axis=0)).then_inc(s_unit[u], 16)

            def weight_round(n):
                if 0 < n <= len(UNITS):
                    share = unit_shares(n - 1)[1]
                    before = overlapped(n - 1)
                    dveF.wait(pool, f"d{n - 1}", 0)
                    poolF.done(pool.tensor_tensor(raw_a[:, share], raw_a[:, share], wd[:, share], ALU.add), f"y{n - 1}")
                    if before is not None:
                        peF.wait(pool, f"t{last_turn(before)}", 0)
                    poolF.wait(pool, f"y{n - 1}", 0)
                    poolF.done(pool.tensor_tensor(wq8[:, share], raw_a[:, share], wd[:, share], ALU.subtract), f"q{n - 1}")
                for u in range(len(UNITS)):
                    before = overlapped(u)
                    if before is not None and before == n - 1:
                        gather(u)

            def iteration(l, p, a, b, o):
                if b is not None:
                    dveB.wait(pool, "ag1", b)
                    apart(pool)
                    poolB.done(pool.tensor_scalar(var_eps2[:, :], mv2[:, :, 1], LN_EPS, None, ALU.add), "ve")
                    poolB.wait(pool, "ve", b)
                    poolB.done(pool.tensor_tensor(rstd2[:, :], var_eps2[:, :], minus_half[:, :], ALU.pow), "rs")
                    dveB.wait(pool, "d", b)
                    poolB.done(pool.tensor_tensor(cx[:, 1, :], cx[:, 1, :], dx[:, 1, :], ALU.add), "y")
                    poolB.wait(pool, "y", b)
                    peB.wait(pool, "qxT", b - 1)
                    apart(pool)
                    poolB.done(pool.tensor_tensor(qx[:, 1, :], cx[:, 1, :], dx[:, 1, :], ALU.subtract), "q")
                if o is not None:
                    poolB.wait(pool, "cp", o)
                    for t in range(TT):
                        dveO.wait(pool, f"y{t}", o)
                        poolO.done(pool.tensor_tensor(ob[:, t, :], yb[:, t, :], ob[:, t, :], ALU.add), f"o{t}")
                if b is not None:
                    dveA.wait(pool, "x1_1", b)
                    store.wait(pool, b - 1)
                    apart(pool)
                    poolB.done(pool.tensor_copy(ob[:, :, :], x1[:, :, :]), "cp")
                between(weight_round, l, "x")
                between(weight_round, l, "k")
                between(weight_round, l, "q")
                between(weight_round, l, "m")
                if a is not None:
                    for c in range(NC):
                        actA.wait(pool, f"e{c}", a)
                        apart(pool)
                        for h, view in (("a", PT[:, c, 0:512].rearrange("p (h s) -> p h s", s=S)[:, :, 0:P]),
                                        ("b", PT[:, c, 512:768].rearrange("p (h s) -> p h s", s=P))):
                            poolA.done(pool.affine_select(out=view, in_=view, compare_op=ALU.is_ge, fill=0.0, base=0,
                                                          pattern=[[0, 2], [1, P]], channel_multiplier=-1), f"sel{c}{h}")
                between(weight_round, l, "e")
                between(weight_round, l, "s")
                between(weight_round, l, "v")
                if b is not None:
                    i = halves(IT)[1]
                    lift, dst = dq[:, 0, i, :], dq[:, 1, i, :]
                    dveB.wait(pool, "D1", b)
                    poolB.done(pool.tensor_tensor(T[:, i, :], T[:, i, :], lift, ALU.add), "Y")
                    poolB.wait(pool, "Y", b)
                    poolB.done(pool.tensor_tensor(dst, T[:, i, :], lift, ALU.subtract), "Q")
                if l is not None:
                    pool_ln(l)
                between(weight_round, l, "end")

            def pool_ln(p):
                dveL.wait(pool, "ag1", p)
                apart(pool)
                poolL.done(pool.tensor_scalar(var_eps[:, :], mv[:, :, 1], LN_EPS, None, ALU.add), "ve")
                poolL.wait(pool, "ve", p)
                poolL.done(pool.tensor_tensor(rstd[:, :], var_eps[:, :], minus_half[:, :], ALU.pow), "rs")
                poolL.done(pool.tensor_scalar(mean_minus[:, :], mv[:, :, 0], -1.0, None, ALU.mult), "nm")
                poolL.wait(pool, "nm", p)
                poolL.done(pool.tensor_tensor(shift[:, :], mean_minus[:, :], rstd[:, :], ALU.mult), "nb")

            pool_ln(0)
            pool.wait_ge(s_index, 16)
            peW.wait(pool, "a9", 0)
            for u, (j, i, k) in enumerate(UNITS):
                if j == 0:
                    gather(u)
            pipeline(pool, iteration, weight_round, lambda: None)

        ring = [wk[0], wk[1], ff[0], ff[1]]
        w_parts = [(WkvTh[:, 512 * j:512 * j + 512], WkvTl[:, 512 * j:512 * j + 512]) for j in range(2)]
        w_parts += [(WqTh[:, k, :], WqTl[:, k, :]) for k in range(KT)]
        w_parts += [(WoTh[:, k, :], WoTl[:, k, :]) for k in range(KT)]

        def w_views(n):
            views = [*w_parts[n], ring[n % 4][:, :]]
            if n == 0 or 2 <= n < 6:
                views = [v.rearrange("p (g c j) -> p g j c", g=KT, j=G) for v in views[:2]] + \
                    [views[2].rearrange("p (g j c) -> p g j c", g=KT, j=G)]
            return views

        @block.tensor
        def _(pe):
            pe.wait_ge(s_const, N_CONST_FIRST)
            pe.wait_ge(s_gates, 32)
            peW.done(pe.matmul(att[0][:, 0:2], ones[0:1, :], gates[0:1, :], start=True, stop=True), "g")
            for n in range(10):
                if n in (0, 2, 6):
                    pe.wait_ge(s_raw[{0: 1, 2: 0, 6: 2}[n]], 16)
                if n >= 4:
                    dveW.wait(pe, f"a{n - 4}", 0)
                for m in range(4):
                    src = raw_kv[:, 4 * n + m, :] if n < 2 else (raw_q if n < 6 else raw_o)[:, m, (n - 2) % 4 * P:(n - 2) % 4 * P + P]
                    last = pe.transpose(ring[n % 4][:, m * P:(m + 1) * P], src, ident[:, :])
                peW.done(last, f"a{n}")
            pe.wait_ge(s_const, N_CONST)

            def products(out_ap, terms, fresh=True):
                for n, (lhs, rhs) in enumerate(terms):
                    last = pe.matmul(out_ap, lhs, rhs, start=(fresh and n == 0), stop=(n == len(terms) - 1),
                                     skip_group_check=not fresh)
                return last

            def transposes(b):
                actL.wait(pe, "xn1", b)
                for j in range(2):
                    w = wkb(f"xT{j}", pe, b)
                    for kk in range(2):
                        for t in range(TT):
                            last = pe.matmul(w[:, kk * S + t * P:kk * S + t * P + P],
                                             xn[:, t, (2 * j + kk) * P:(2 * j + kk + 1) * P], ident[:, :],
                                             start=(kk == t == 0), stop=True, is_transpose=True, skip_group_check=True)
                    peP.done(last, f"xT{j}")

            def transpose_context(b):
                load_x.wait(pe, b)
                w = wkb("cT", pe, b)
                for t in range(TT):
                    last = pe.matmul(w[:, t * P:(t + 1) * P], cin[:, t, :], ident[:, :],
                                     start=(t == 0), stop=True, is_transpose=True, skip_group_check=True)
                peP.done(last, "cT")

            def less_high(b, *uses):
                for use in uses:
                    high = {"x": xTh, "c": cTh, "k": kh, "q": qh}[use[0]]
                    high = high[:, :] if use == "cT" else flat2(high, int(use[-1]))
                    actP.wait(pe, use, b)
                    peP.done(pe.matmul(wkb(use)[:, 0:high.shape[-1]], minus_identb[:, :], high, start=False, stop=True,
                                       skip_group_check=True), f"{use}m")

            def keys(b, j):
                if j == 0:
                    actP.wait(pe, "cTl", b)
                w = wkb(f"k{j}", pe, b)
                for mm in range(2):
                    m = slice((2 * j + mm) * P, (2 * j + mm + 1) * P)
                    last = products(w[:, mm * S:(mm + 1) * S],
                                    [(WkvTh[:, m], cTh[:, :]), (WkvTh[:, m], cTl[:, :]), (WkvTl[:, m], cTh[:, :])],
                                    fresh=(mm == 0))
                peP.done(last, f"k{j}")

            def queries(b, j, part=0, parts=1):
                if j == 0:
                    actP.wait(pe, "xT1l", b)
                w = wkb(f"q{j}", pe if part == 0 else None, b)
                each = [(mm, n) for mm in range(2) for n in range(3 * KT)]
                for mm, n in each[part * len(each) // parts:(part + 1) * len(each) // parts]:
                    m = slice((2 * j + mm) * P, (2 * j + mm + 1) * P)
                    k, (a, c) = n // 3, ((WqTh, xTh), (WqTh, xTl), (WqTl, xTh))[n % 3]
                    last = pe.matmul(w[:, mm * S:(mm + 1) * S], a[:, k, m], c[:, k, :], start=(mm == n == 0),
                                     stop=(n == 3 * KT - 1), skip_group_check=True)
                if part == parts - 1:
                    peP.done(last, f"q{j}")

            def values(b):
                for t in range(TT):
                    w = wkb(f"v{t}", pe, b)
                    tok = slice(t * P, (t + 1) * P)
                    peP.done(products(w[:, :], [(cTh[:, tok], WkvTh[:, H:]), (cTh[:, tok], WkvTl[:, H:]),
                                                (cTl[:, tok], WkvTh[:, H:])]), f"v{t}")

            def scores(b, c):
                if c == 0:
                    stack_k.wait(pe, b)
                    stack_q.wait(pe, b)
                if c >= 2:
                    (dveS if c < 4 else dveA).wait(pe, f"mx{c - 2}b", b)
                else:
                    actA.wait(pe, f"e{NC - 2 + c}", b - 1)
                w = att[c % 2]
                pe.matmul(w[:, 0:512], identb[:, :], causal4[:, :, :].rearrange("p a k -> p (a k)"),
                          start=True, stop=False, skip_group_check=True)
                for h in range(2):
                    at = place(2 * c + h)
                    q0, q1 = Q4[:, at, 0:P], Q4[:, at, P:S]
                    k0, k1 = K4[:, at, 0:P], K4[:, at, P:S]
                    pe.matmul(w[:, h * P:(h + 1) * P], q0, k0, start=False, stop=True, skip_group_check=True)
                    pe.matmul(w[:, (2 + h) * P:(3 + h) * P], q1, k1, start=False, stop=True, skip_group_check=True)
                    last = pe.matmul(w[:, (4 + h) * P:(5 + h) * P], q1, k0, start=True, stop=True)
                (peS if c < 2 else peA).done(last, f"S{c}")

            def shifted(b, c):
                if c == 0:
                    stack_m.wait(pe, b)
                if c >= 2:
                    actA.wait(pe, f"e{c - 2}", b)
                else:
                    dveA.wait(pe, f"mx{NC - 2 + c}b", b)
                w = att[c % 2]
                for h in range(2):
                    head = place(2 * c + h)
                    pe.matmul(w[:, h * S:(h + 1) * S], K4[:, head, 0:P], Q4[:, head, :], start=True, stop=True)
                    last = pe.matmul(w[:, (4 + h) * P:(5 + h) * P], K4[:, head, P:S], Q4[:, head, P:S], start=True, stop=True)
                peA.done(last, f"ST{c}")

            def weighted(b, g):
                w = wkb(f"PV{g}", pe, b)
                if g == 0:
                    actP.wait(pe, "v1", b)
                poolA.wait(pe, f"sel{2 * g + 1}b", b)
                for t in range(TT):
                    for j in range(G):
                        c, h = 2 * g + j // 2, j % 2
                        p = PT[:, c, h * S:(h + 1) * S] if t == 0 else PT[:, c, (4 + h) * P:(5 + h) * P]
                        last = pe.matmul(w[HD * j:HD * j + HD, t * P:S], V[:, t, (G * g + j) * HD:(G * g + j + 1) * HD], p,
                                         start=(t == 0), stop=(t == TT - 1), skip_group_check=True)
                peA.done(last, f"PV{g}")

            def sums(b):
                w = wkb("sum", pe, b)
                for g in range(KT):
                    for t in range(TT):
                        for j in range(G):
                            c, h = 2 * g + j // 2, j % 2
                            p = PT[:, c, h * S:(h + 1) * S] if t == 0 else PT[:, c, (4 + h) * P:(5 + h) * P]
                            last = pe.matmul(w[HD * j:HD * j + HD, t * P:S], pick[:, g, :], p, start=(g == 0 and t == 0),
                                             stop=(g == KT - 1 and t == TT - 1), skip_group_check=True)
                peA.done(last, "sum")

            def projected(b, t):
                if t == 0:
                    actA.wait(pe, "oh1", b)
                    dveA.wait(pe, "ol1", b)
                w = wkb(f"wo{t}", pe, b)
                tok = slice(t * P, (t + 1) * P)
                peA.done(products(w[:, :], [(a[:, g, tok], c[:, g, :]) for g in range(KT)
                                            for a, c in ((oh, WoTh), (oh, WoTl), (ol, WoTh))]), f"wo{t}")

            def mlp_in(b):
                dveB.wait(pe, "q", b)
                poolB.wait(pe, "q", b)
                w = ffb("qxT", pe, b)[:, :].bitcast(BF16)
                for k in range(KT):
                    for t in range(TT):
                        last = pe.transpose(w[:, k * S + t * P:k * S + t * P + P], qx[:, t, k * P:(k + 1) * P], identb[:, :])
                peB.done(last, "qxT")

            def mlp_in_scales(b):
                dveB.wait(pe, "sp1", b)
                w = ffb("sxb", pe, b)
                for t in range(TT):
                    last = pe.matmul(w[:, t * P:(t + 1) * P], spread[:, t, :], ident[:, :], start=True, stop=True)
                peB.done(last, "sxb")

            def mlp_products(b, use, W, j):
                w = ffb(f"{use}{j}", pe, b)
                for u, n in enumerate(PAIRS[j]):
                    i = slice(n * P, (n + 1) * P)
                    last = products(w[:, u * S:(u + 1) * S], [(W[:, k, i], qxT[:, k, :]) for k in range(KT)])
                peB.done(last, f"{use}{j}")

            def row_max(b):
                dveB.wait(pe, "ac1", b)
                w = ffb("amT", pe, b)
                for t in range(TT):
                    for n in range(2):
                        last = pe.transpose(w[:, (2 * t + n) * P:(2 * t + n + 1) * P], tmax[:, n, t * P:(t + 1) * P],
                                            ident[:, :])
                peB.done(last, "amT")

            def row_inv(b):
                dveB.wait(pe, "sq1", b)
                w = ffb("invb", pe, b)
                for t in range(TT):
                    last = pe.matmul(w[:, t * P:(t + 1) * P], spread2[:, t, :], ident[:, :], start=True, stop=True)
                peB.done(last, "invb")

            def down(b, h):
                half = halves(IT)[h]
                (dveB, poolB)[h].wait(pe, "Q", b)
                for t in range(TT):
                    w = ffb(f"dn{t}", pe if h == 0 else None, b)
                    for i in range(half.start, half.stop):
                        last = pe.matmul(w[:, :], dq[:, 1, i, t * P:(t + 1) * P], WdT[:, i, :],
                                         start=(i == 0), stop=(i == IT - 1))
                    if h == 1:
                        peB.done(last, f"dn{t}")

            def iteration(l, p, a, b, o):
                if p is not None:
                    transposes(p)
                if a is not None:
                    scores(a, 2)
                if p is not None:
                    less_high(p, "xT0", "xT1")
                    transpose_context(p)
                if a is not None:
                    scores(a, 3)
                if p is not None:
                    less_high(p, "cT")
                if o is not None:
                    down(o, 1)
                between(weight_round, l, "x")
                if p is not None:
                    keys(p, 0)
                    keys(p, 1)
                if a is not None:
                    scores(a, 4)
                if p is not None:
                    less_high(p, "k0", "k1")
                between(weight_round, l, "k")
                if b is not None:
                    mlp_in(b)
                    mlp_in_scales(b)
                between(weight_round, l, "q")
                if p is not None:
                    queries(p, 0, 0, 4)
                if b is not None:
                    actB.wait(pe, "qxT", b)
                for n in range(len(PAIRS) + 1):
                    if b is not None and n < len(PAIRS):
                        mlp_products(b, "ga", WgT, n)
                    if b is not None and n > 0:
                        mlp_products(b, "up", WuT, n - 1)
                    if a is not None and n + 5 < NC:
                        scores(a, n + 5)
                    if p is not None:
                        if n < 3:
                            queries(p, 0, n + 1, 4)
                        if n == 3:
                            less_high(p, "q0")
                        for part in {3: (0,), 4: (1, 2), 5: (3,)}.get(n, ()):
                            queries(p, 1, part, 4)
                    if a is not None and n == 4:
                        dveA.wait(pe, "m3", a)
                        w = wkb("mT", pe, a)[0:3 * TT * NH, 0:P // 2].bitcast(BF16)
                        peA.done(pe.transpose(w, m_parts[:, :, :].rearrange("p r n -> p (r n)"), identb[:, :]), "mT")
                between(weight_round, l, "m")
                if a is not None:
                    shifted(a, 0)
                    shifted(a, 1)
                if p is not None:
                    less_high(p, "q1")
                if a is not None:
                    shifted(a, 2)
                if b is not None:
                    row_max(b)
                if a is not None:
                    shifted(a, 3)
                    shifted(a, 4)
                    shifted(a, 5)
                if b is not None:
                    row_inv(b)
                between(weight_round, l, "e")
                if a is not None:
                    weighted(a, 0)
                    shifted(a, 6)
                    shifted(a, 7)
                    weighted(a, 1)
                    weighted(a, 2)
                    weighted(a, 3)
                    sums(a)
                between(weight_round, l, "s")
                if b is not None:
                    down(b, 0)
                if p is not None:
                    values(p)
                between(weight_round, l, "v")
                if p is not None:
                    scores(p, 0)
                    scores(p, 1)
                if a is not None:
                    projected(a, 0)
                    projected(a, 1)
                between(weight_round, l, "end")

            def weight_round(n):
                for turn, (u, i, k) in enumerate(TURNS):
                    if u != n - 2:
                        continue
                    j, m, _ = UNITS[u]
                    dveF.wait(pe, f"q{u}", 0)
                    poolF.wait(pe, f"q{u}", 0)
                    if turn >= 2:
                        actF.wait(pe, f"t{turn - 2}", 0)
                    w = ff[turn % 2][:, :].bitcast(BF16)
                    for a in range(k):
                        if j == 2:
                            last = pe.transpose(w[:, a * P:(a + 1) * P], wq8[:, m * I + (i + a) * P:m * I + (i + a + 1) * P],
                                                identb[:, :])
                            continue
                        for c in range(KT):
                            last = pe.transpose(w[:, (c * k + a) * P:(c * k + a + 1) * P],
                                                wq8[:, (i + a) * H + c * P:(i + a) * H + (c + 1) * P], identb[:, :])
                    peF.done(last, f"t{turn}")

            def last_weights():
                dveF.wait(pe, "spread", 0)
                actF.wait(pe, f"t{len(TURNS) - 2}", 0)
                for m in range(KT):
                    last = pe.matmul(ff[0][:, m * P:(m + 1) * P], cx[:, 0, m * P:(m + 1) * P], ident[:, :], start=True, stop=True)
                peF.done(last, "sc")
                dveF.wait(pe, "dsc", 0)

            pipeline(pe, iteration, weight_round, last_weights)

        @block.scalar
        def _(act):
            def copy(dst, src):
                return act.activation(dst, src, ACT.Copy)

            peW.wait(act, "g", 0)
            actW.done(act.activation(tanh_g[:, :], att[0][:, 0:2], ACT.Tanh), "tanh")
            for n in range(10):
                peW.wait(act, f"a{n}", 0)
                high_part, _, w = w_views(n)
                actW.done(copy(high_part, w), f"a{n}")

            def take(b, progress, pe_progress, use, w, dst):
                pe_progress.wait(act, use, b)
                progress.done(copy(dst, w), use)

            def lift(progress, dve_progress, ready, value, dst, step, b):
                dve_progress.wait(act, ready, b)
                progress.done(act.activation(dst, value, ACT.Abs, scale=ROUND_LIFT), step)

            def high(b, use, w, dst):
                take(b, actP, peP, use, w, dst)

            def low(b, use, w, dst):
                peP.wait(act, f"{use}m", b)
                actP.done(copy(dst, w), f"{use}l")

            def both(b, uses, highs, lows):
                for part, dst in ((high, highs), (low, lows)):
                    for use in uses if dst is not None else ():
                        part(b, use, wkb(use)[:, :], flat2(dst, int(use[-1])))

            def project(b):
                peP.wait(act, "q1m", b - 1)
                both(b, ("xT0", "xT1"), xTh, None)

            def project_context(b):
                peP.wait(act, "v1", b - 1)
                high(b, "cT", wkb("cT")[:, 0:S], cTh[:, :])
                low(b, "cT", wkb("cT")[:, 0:S], cTl[:, :])

            def project_q(b, part, j):
                if part is high and j == 0:
                    stack_q.wait(act, b - 1)
                part(b, f"q{j}", wkb(f"q{j}")[:, :], flat2(qh if part is high else ql, j))

            def norm1(b):
                peP.wait(act, "xT1", b - 1)
                poolL.wait(act, "nb", b)
                for t in range(TT):
                    actL.done(act.activation(xn[:, t, :], xin[:, t, :], ACT.Identity, bias=shift[:, t:t + 1],
                                             scale=rstd[:, t:t + 1]), f"xn{t}")

            def norm2_centred(b, t):
                dveA.wait(act, f"x1_{t}", b)
                dveB.wait(act, f"nm{t}", b)
                dveB.wait(act, "q", b - 1)
                poolB.wait(act, "q", b - 1)
                actB.done(act.activation(cx[:, t, :], x1[:, t, :], ACT.Identity, bias=mean_minus2[:, t:t + 1]), f"c{t}")

            def project_v(b, t):
                high(b, f"v{t}", wkb(f"v{t}")[:, :], V[:, t, :])

            def exps(b, c):
                if c == 0:
                    peA.wait(act, "sum", b - 1)
                peA.wait(act, f"ST{c}", b)
                actA.done(act.activation(PT[:, c, :], att[c % 2][:, 0:768], ACT.Exp, scale=SCALE), f"e{c}")

            def take_o(b, g):
                if g == 0:
                    dveA.wait(act, "on1", b - 1)
                peA.wait(act, f"PV{g}", b)
                actA.done(copy(O[:, g, :], wkb(f"PV{g}")[:, 0:S]), f"O{g}")

            def lift_half(b, h):
                i = halves(IT)[h]
                (dveB, poolB)[h].wait(act, "Q", b - 1)
                lift(actB, dveB, f"X{h}", T[:, i, :], dq[:, 0, i, :], f"absT{h}", b)

            def iteration(l, p, a, b, o):
                if p is not None:
                    project(p)
                if b is not None:
                    norm2_centred(b, 1)
                if p is not None:
                    both(p, ("xT0", "xT1"), None, xTl)
                    project_context(p)
                between(weight_round, l, "x")
                if b is not None:
                    poolB.wait(act, "q", b - 1)
                    lift(actB, dveB, "x1", cx[:, :, :], dx[:, :, :], "absx", b)
                if p is not None:
                    stack_k.wait(act, p - 1)
                    both(p, ("k0", "k1"), kh, kl)
                between(weight_round, l, "k")
                if b is not None:
                    peB.wait(act, f"up{len(PAIRS) - 1}", b - 1)
                    take(b, actB, peB, "qxT", ffb("qxT")[:, :].bitcast(BF16), qxT[:, :, :].rearrange("p k s -> p (k s)"))
                between(weight_round, l, "q")
                if b is not None:
                    dveB.wait(act, f"gs{IT - 1}", b - 1)
                    take(b, actB, peB, "sxb", ffb("sxb")[:, 0:S], sxb[:, :])
                for n, pair in enumerate(PAIRS):
                    if b is not None:
                        dveB.wait(act, f"gs{pair[-1]}", b)
                        if n >= 2:
                            dveB.wait(act, f"t{PAIRS[n - 2][-1]}", b)
                        at = slice(pair[0] % 4, pair[0] % 4 + len(pair))
                        actB.done(act.activation(sl[:, at, :], gs[:, at, :], ACT.Silu), f"silu{n}")
                    if p is not None and n in (2, 3, 5):
                        project_q(p, (high, low)[n == 3], n // 5)
                    if a is not None and n == 4:
                        stack_m.wait(act, a - 1)
                        take(a, actA, peA, "mT", wkb("mT")[0:3 * TT * NH, 0:P // 2].bitcast(BF16), mT[:, :])
                between(weight_round, l, "m")
                if a is not None:
                    exps(a, 0)
                    exps(a, 1)
                if p is not None:
                    project_q(p, low, 1)
                if a is not None:
                    for c in range(2, 6):
                        exps(a, c)
                between(weight_round, l, "e")
                if a is not None:
                    take_o(a, 0)
                    exps(a, 6)
                    exps(a, 7)
                    take_o(a, 1)
                if b is not None:
                    lift_half(b, 0)
                if a is not None:
                    take_o(a, 2)
                if b is not None:
                    lift_half(b, 1)
                if a is not None:
                    take_o(a, 3)
                between(weight_round, l, "s")
                if p is not None:
                    peA.wait(act, "PV3", p - 1)
                    project_v(p, 0)
                if a is not None:
                    peA.wait(act, "wo1", a - 1)
                    for h in range(2):
                        dveA.wait(act, f"on{h}", a)
                        actA.done(copy(oh[:, 2 * h:2 * h + 2, :], R[:, 2 * h:2 * h + 2, :]), f"oh{h}")
                if p is not None:
                    project_v(p, 1)
                between(weight_round, l, "v")
                if l is not None:
                    norm1(l)
                between(weight_round, l, "end")
                if a is not None:
                    if isinstance(l, int) and l == 2:
                        dveF.wait(act, "dsc", 0)
                    norm2_centred(a, 0)

            def weight_round(n):
                if n < len(UNITS):
                    j, i, k = UNITS[n]
                    span, tiles = unit_span(n)
                    before = overlapped(n)
                    if before is not None:
                        dveF.wait(act, f"q{before}", 0)
                        poolF.wait(act, f"q{before}", 0)
                    dveF.wait(act, f"lf{n}", 0)
                    for m, tile in enumerate(tiles):
                        last = act.activation(wd[:, tile], raw_a[:, tile], ACT.Abs, scale=wlift[:, j, i + m:i + m + 1])
                    actF.done(last, f"lift{n}")
                    actF.wait(act, f"lift{n}", 0)
                    for m, tile in enumerate(tiles):
                        last = act.activation(raw_a[:, tile], raw_a[:, tile], ACT.Copy, scale=winv[:, j, i + m:i + m + 1])
                    actF.done(last, f"x{n}")
                for turn, (u, i, k) in enumerate(TURNS):
                    if u != n - 2:
                        continue
                    j, m, _ = UNITS[u]
                    peF.wait(act, f"t{turn}", 0)
                    w = ff[turn % 2][:, :].bitcast(BF16)
                    if j < 2:
                        dst = (WgT, WuT)[j][:, :, i * P:(i + k) * P]
                        src = w[:, 0:KT * k * P].rearrange("p (m f) -> p m f", m=KT)
                    else:
                        dst, src = WdT[:, i:i + k, m * P:(m + 1) * P], w[:, 0:k * P].rearrange("p (i o) -> p i o", i=k)
                    actF.done(copy(dst, src), f"t{turn}")

            norm1(0)
            pipeline(act, iteration, weight_round, lambda: None)

        @block.vector
        def _(dve):
            def low(dst, w, high):
                return dve.tensor_tensor(dst, w, high, ALU.subtract)

            for n in range(10):
                actW.wait(dve, f"a{n}", 0)
                high_part, low_part, w = w_views(n)
                dveW.done(low(low_part, w, high_part), f"a{n}")

            def floored(progress, b, lift, d):
                progress.done(dve.tensor_scalar(lift, lift, ROUND_FLOOR * ROUND_LIFT, None, ALU.max), d)

            def lifted(progress, b, value, lift, d, y):
                progress.wait(dve, d, b)
                progress.done(dve.tensor_tensor(value, value, lift, ALU.add), y)

            def rounded(progress, b, value, lift, dst, y, q):
                progress.wait(dve, y, b)
                progress.done(dve.tensor_tensor(dst, value, lift, ALU.subtract), q)

            def weight_round(n):
                if n < len(UNITS):
                    j, i, k = UNITS[n]
                    span, tiles = unit_span(n)
                    rows = slice(i, i + k)
                    dve.wait_ge(s_unit[n], 16 * (k if j < 2 else 1))
                    dveF.done(dve.tensor_reduce(wmax[:, j, rows], raw_a[:, span].rearrange("p (n f) -> p n f", n=k), AX.X,
                                                ALU.max, apply_absolute_value=True), f"mx{n}")
                    dveF.wait(dve, f"mx{n}", 0)
                    dveF.done(dve.reciprocal(winv[:, j, rows], wmax[:, j, rows]), f"rc{n}")
                    dveF.wait(dve, f"rc{n}", 0)
                    dveF.done(dve.tensor_scalar(winv[:, j, rows], winv[:, j, rows], FP8_MAX, None, ALU.mult), f"iv{n}")
                    dveF.wait(dve, f"iv{n}", 0)
                    dveF.done(dve.tensor_scalar(wlift[:, j, rows], winv[:, j, rows], ROUND_LIFT, None, ALU.mult), f"lf{n}")
                    dveF.done(dve.tensor_scalar(wscale[:, j, rows], wmax[:, j, rows], 1.0 / FP8_MAX, None, ALU.mult), f"sc{n}")
                if 0 < n <= len(UNITS):
                    u = n - 1
                    span, share = unit_span(u)[0], unit_shares(u)[0]
                    before = overlapped(u)
                    actF.wait(dve, f"x{u}", 0)
                    floored(dveF, 0, wd[:, span], f"d{u}")
                    lifted(dveF, 0, raw_a[:, share], wd[:, share], f"d{u}", f"y{u}")
                    if before is not None:
                        peF.wait(dve, f"t{last_turn(before)}", 0)
                    rounded(dveF, 0, raw_a[:, share], wd[:, share], wq8[:, share], f"y{u}", f"q{u}")

            def norm1_stats(b, t):
                load_x.wait(dve, b)
                dveL.done(dve.bn_stats(bn[:, t, :], xin[:, t, :]), f"st{t}")

            def norm1_mean(b):
                for t in range(TT):
                    dveL.wait(dve, f"st{t}", b)
                    apart(dve)
                    dveL.done(dve.bn_aggr(mv[:, t, :], bn[:, t, :]), f"ag{t}")

            def maxima(b, c):
                (peS if c < 2 else peA).wait(dve, f"S{c}", b)
                progress = dveS if c < 2 else dveA
                heads = slice(place(2 * c), place(2 * c + 1) + 1, KT)
                w = att[c % 2]
                progress.done(dve.tensor_reduce(mx[:, heads, 0], w[:, 0:2 * P].rearrange("p (h k) -> p h k", h=2),
                                            AX.X, ALU.max), f"mx{c}a")
                progress.done(dve.tensor_reduce(mx[:, heads, 1],
                                            w[:, 2 * P:6 * P].rearrange("p (r h k) -> p h r k", r=2, h=2),
                                            AX.XY, ALU.max), f"mx{c}b")

            def max_parts(b):
                dveA.wait(dve, f"mx{NC - 1}b", b)
                m = mx[:, :, :].rearrange("p h t -> p (h t)")
                dveA.done(dve.tensor_scalar(m_parts[:, 0, :], m, -1.0, None, ALU.mult), "m1")
                dveA.wait(dve, "m1", b)
                dveA.done(dve.scalar_tensor_tensor(out=m_rest[:, 0, :], in0=m, scalar=-1.0, in1=m_parts[:, 0, :],
                                                   op0=ALU.mult, op1=ALU.subtract), "r1")
                dveA.wait(dve, "r1", b)
                dveA.done(dve.tensor_copy(m_parts[:, 1, :], m_rest[:, 0, :]), "m2")
                dveA.wait(dve, "m2", b)
                dveA.done(dve.tensor_tensor(m_parts[:, 2, :], m_rest[:, 0, :], m_parts[:, 1, :], ALU.subtract), "m3")

            def normalise(b):
                peA.wait(dve, "sum", b)
                dveA.done(dve.reciprocal(rsum[:, :], wkb("sum")[:, 0:S]), "rc")
                dveA.wait(dve, "rc", b)
                apart(dve)
                for g in range(KT):
                    dveA.done(dve.stream_shuffle(out=R[:, g, :], in_=rsum[:, :], mask=[g] * HD), f"sh{g}")
                actA.wait(dve, "O3", b)
                dveA.wait(dve, "sh3", b)
                for h in range(2):
                    g = slice(2 * h, 2 * h + 2)
                    dveA.done(dve.tensor_tensor(R[:, g, :], O[:, g, :], R[:, g, :], ALU.mult), f"on{h}")

            def normalised_low(b):
                for h in range(2):
                    g = slice(2 * h, 2 * h + 2)
                    actA.wait(dve, f"oh{h}", b)
                    dveA.done(low(ol[:, g, :], R[:, g, :], oh[:, g, :]), f"ol{h}")

            def residual(b, t):
                if t == 0:
                    load_res.wait(dve, b)
                    poolB.wait(dve, "cp", b - 1)
                    actB.wait(dve, "c1", b - 1)
                peA.wait(dve, f"wo{t}", b)
                dveA.done(dve.scalar_tensor_tensor(out=x1[:, t, :], in0=wkb(f"wo{t}")[:, :], scalar=tanh_g[:, 0:1],
                                                   in1=xres[:, t, :], op0=ALU.mult, op1=ALU.add), f"x1_{t}")

            def norm2_stats(b, t):
                dveA.wait(dve, f"x1_{t}", b)
                dveB.done(dve.bn_stats(bn2[:, t, :], x1[:, t, :]), f"st{t}")
                dveB.wait(dve, f"st{t}", b)
                apart(dve)
                dveB.done(dve.bn_aggr(mv2[:, t, :], bn2[:, t, :]), f"ag{t}")
                dveB.wait(dve, f"ag{t}", b)
                dveB.done(dve.tensor_scalar(mean_minus2[:, t:t + 1], mv2[:, t, 0:1], -1.0, None, ALU.mult), f"nm{t}")

            def norm2_scales(b):
                for t in range(TT):
                    actB.wait(dve, f"c{t}", b)
                    dveB.done(dve.tensor_reduce(amax[:, t:t + 1], cx[:, t, :], AX.X, ALU.max, apply_absolute_value=True),
                              f"am{t}")
                dveB.wait(dve, "am1", b)
                dveB.done(dve.reciprocal(ainv[:, :], amax[:, :]), "rc")
                dveB.wait(dve, "rc", b)
                for t in range(TT):
                    dveB.done(dve.tensor_scalar(cx[:, t, :], cx[:, t, :], ainv[:, t:t + 1], FP8_MAX, ALU.mult, ALU.mult), f"x{t}")
                poolB.wait(dve, "rs", b)
                dveB.done(dve.tensor_tensor(sx[:, :], amax[:, :], rstd2[:, :], ALU.mult), "sx0")
                dveB.wait(dve, "sx0", b)
                dveB.done(dve.tensor_scalar(sx[:, :], sx[:, :], 1.0 / FP8_MAX, None, ALU.mult), "sx1")

            def norm2_fp8(b):
                peB.wait(dve, "qxT", b - 1)
                actB.wait(dve, "absx", b)
                floored(dveB, b, dx[:, :, :], "d")
                lifted(dveB, b, cx[:, 0, :], dx[:, 0, :], "d", "y")
                rounded(dveB, b, cx[:, 0, :], dx[:, 0, :], qx[:, 0, :], "y", "q")
                peB.wait(dve, "sxb", b - 1)
                for t in range(TT):
                    dveB.done(dve.tensor_scalar(spread[:, t, :], ones[:, :], sx[:, t:t + 1], None, ALU.mult), f"sp{t}")

            def gate(b, n):
                if n == 0:
                    actB.wait(dve, "sxb", b)
                if n % 2 == 0:
                    peB.wait(dve, f"ga{n // 2}", b)
                    if n >= 4:
                        actB.wait(dve, f"silu{n // 2 - 2}", b)
                dveB.done(dve.scalar_tensor_tensor(out=gs[:, n % 4, :], in0=ffb(f"ga{n // 2}")[:, n % 2 * S:(n % 2 + 1) * S],
                                                   scalar=wscale[:, 0, n:n + 1], in1=sxb[:, :], op0=ALU.mult, op1=ALU.mult),
                          f"gs{n}")

            def up(b, n):
                if n == 0:
                    peB.wait(dve, "dn1", b - 1)
                if n % 2 == 0:
                    peB.wait(dve, f"up{n // 2}", b)
                    actB.wait(dve, f"silu{n // 2}", b)
                dveB.done(dve.scalar_tensor_tensor(out=T[:, n, :], in0=ffb(f"up{n // 2}")[:, n % 2 * S:(n % 2 + 1) * S],
                                                   scalar=wscale[:, 1, n:n + 1], in1=sl[:, n % 4, :], op0=ALU.mult, op1=ALU.mult),
                          f"t{n}")

            def largest(b, n):
                first, last = [(h.start, h.stop) for h in halves(IT)][n]
                dveB.wait(dve, f"t{last - 1}", b)
                if n == 0:
                    peB.wait(dve, "amT", b - 1)
                dveB.done(dve.tensor_reduce(tmax[:, n, :], T[:, first:last, :].rearrange("p i s -> p s i"), AX.X, ALU.max,
                                            apply_absolute_value=True), f"ac{n}")

            def mlp_scales(b):
                peB.wait(dve, "amT", b)
                dveB.done(dve.tensor_reduce(tm[:, :], ffb("amT")[:, :].rearrange("p (t i) -> p t i", t=TT), AX.X, ALU.max), "mt")
                dveB.wait(dve, "mt", b)
                dveB.done(dve.reciprocal(tinv[:, :], tm[:, :]), "rc2")
                dveB.wait(dve, "rc2", b)
                peB.wait(dve, "invb", b - 1)
                for t in range(TT):
                    dveB.done(dve.tensor_scalar(spread2[:, t, :], ones[:, :], tinv[:, t:t + 1], FP8_MAX, ALU.mult, ALU.mult),
                              f"sq{t}")
                dveB.done(dve.tensor_tensor(st[:, :], tm[:, :], sx[:, :], ALU.mult), "st_a")
                dveB.wait(dve, "st_a", b)
                dveB.done(dve.tensor_scalar(st[:, :], st[:, :], 1.0 / FP8_MAX, None, ALU.mult), "st_b")

            def mlp_scaled(b):
                peB.wait(dve, "invb", b)
                dveB.wait(dve, "ac1", b)
                for h, i in enumerate(halves(IT)):
                    inv = ffb("invb")[:, 0:S].unsqueeze(1).to_broadcast([P, i.stop - i.start, S])
                    dveB.done(dve.tensor_tensor(T[:, i, :], T[:, i, :], inv, ALU.mult), f"X{h}")

            def mlp_floored(b, h):
                i = halves(IT)[h]
                actB.wait(dve, f"absT{h}", b)
                floored(dveB, b, dq[:, 0, i, :], f"D{h}")

            def mlp_lifted(b):
                i = halves(IT)[0]
                lifted(dveB, b, T[:, i, :], dq[:, 0, i, :], "D0", "Y")

            def mlp_rounded(b):
                i = halves(IT)[0]
                rounded(dveB, b, T[:, i, :], dq[:, 0, i, :], dq[:, 1, i, :], "Y", "Q")

            def mlp_out(b, t):
                peB.wait(dve, f"dn{t}", b)
                poolO.wait(dve, f"o{t}", b - 1)
                dveO.done(dve.scalar_tensor_tensor(out=yb[:, t, :], in0=ffb(f"dn{t}")[:, :], scalar=st[:, t:t + 1],
                                                   in1=down_scale[:, :], op0=ALU.mult, op1=ALU.mult), f"y{t}")

            def iteration(l, p, a, b, o):
                if a is not None:
                    maxima(a, 2)
                between(weight_round, l, "x")
                if b is not None:
                    norm2_scales(b)
                if a is not None:
                    maxima(a, 3)
                between(weight_round, l, "k")
                if b is not None:
                    norm2_fp8(b)
                if o is not None:
                    mlp_out(o, 0)
                    mlp_out(o, 1)
                between(weight_round, l, "q")
                if a is not None:
                    maxima(a, 4)
                for n in range(len(PAIRS) + 1):
                    if b is not None:
                        for step, m in mlp_order(IT, n):
                            {"gs": gate, "t": up, "ac": largest}[step](b, m)
                    if a is not None and n + 5 < NC:
                        maxima(a, n + 5)
                    if a is not None and n == NC - 6:
                        max_parts(a)
                between(weight_round, l, "m")
                if l is not None:
                    norm1_stats(l, 0)
                if b is not None:
                    mlp_scales(b)
                    mlp_scaled(b)
                if l is not None:
                    norm1_stats(l, 1)
                if b is not None:
                    mlp_floored(b, 0)
                    mlp_lifted(b)
                    mlp_floored(b, 1)
                    mlp_rounded(b)
                between(weight_round, l, "e")
                between(weight_round, l, "s")
                if a is not None:
                    normalise(a)
                    normalised_low(a)
                if l is not None:
                    norm1_mean(l)
                between(weight_round, l, "v")
                if p is not None:
                    maxima(p, 0)
                    maxima(p, 1)
                if a is not None:
                    residual(a, 0)
                    norm2_stats(a, 0)
                    residual(a, 1)
                    norm2_stats(a, 1)
                between(weight_round, l, "end")

            def last_weights():
                dveF.wait(dve, f"q{len(UNITS) - 1}", 0)
                poolF.wait(dve, f"q{len(UNITS) - 1}", 0)
                for m in range(KT):
                    last = dve.tensor_scalar(cx[:, 0, m * P:(m + 1) * P], ones[:, :], wscale[:, 2, m:m + 1], None, ALU.mult)
                dveF.done(last, "spread")
                peF.wait(dve, "sc", 0)
                actW.wait(dve, "tanh", 0)
                dveF.done(dve.tensor_scalar(down_scale[:, :], ff[0][:, :], tanh_g[:, 1:2], None, ALU.mult), "dsc")
                dveF.wait(dve, "dsc", 0)

            dve.wait_ge(s_const, N_CONST)
            norm1_stats(0, 0)
            norm1_stats(0, 1)
            norm1_mean(0)
            pipeline(dve, iteration, weight_round, last_weights)


def halves(n_tiles):
    return slice(0, (n_tiles + 1) // 2), slice((n_tiles + 1) // 2, n_tiles)


def pairs(n_tiles):
    return [tuple(range(n, min(n + 2, n_tiles))) for n in range(0, n_tiles, 2)]


def weight_steps(n_units, scale, rounding):
    return [f"{s}{n}" for r in range(n_units + 1) for n, steps in ((r, scale), (r - 1, rounding)) if 0 <= n < n_units
            for s in steps]


def gate_up_steps(n_pairs):
    return [s for n in range(n_pairs + 1) for s in ([f"ga{n}"] if n < n_pairs else []) + ([f"up{n - 1}"] if n else [])]


def mlp_order(n_tiles, n):
    tiles = pairs(n_tiles)
    order = [("gs", m) for m in (tiles[n] if n < len(tiles) else ())] + [("t", m) for m in (tiles[n - 1] if n else ())]
    return order + [("ac", h) for h, half in enumerate(halves(n_tiles)) if ("t", half.stop - 1) in order]


def mlp_steps(n_tiles):
    return [f"{s}{m}" for n in range(len(pairs(n_tiles)) + 1) for s, m in mlp_order(n_tiles, n)]


_INS = ["x", "ctx_512", "g_xattn", "g_ffn", "L0_xattn_Wq", "L0_xattn_Wkv_expand", "L0_xattn_Wout",
        "L0_ffn_w_gate", "L0_ffn_w_up", "L0_ffn_w_down", "L0_ffn_down_reorder_index"]


def kernel(**inputs):
    import numpy as _np
    import concourse.bacc as _bacc
    from concourse import mybir as _mybir
    from concourse.bass_utils import run_bass_kernel_spmd as _run

    nc = _bacc.Bacc("TRN2", target_bir_lowering=False, num_devices=1)
    arrays, args = {}, []
    for name in _INS:
        a = _np.ascontiguousarray(inputs[name])
        arrays[f"in_{name}_dram"] = a
        args.append(nc.dram_tensor(f"in_{name}_dram", a.shape, _mybir.dt.from_np(a.dtype), kind="ExternalInput").ap())
    args.append(nc.dram_tensor("out_0_dram", inputs["x"].shape, F32, kind="ExternalOutput").ap())
    gated_block_kernel(nc, *args)
    r = _run(nc, [arrays], core_ids=[0])
    return r.results[0]["out_0_dram"]
```
